# Optimizing a Trainium2 kernel written in Bass

```python
import numpy as np
import jax
import jax.numpy as jnp

def _softmax(x, axis=-1):
    return jax.nn.softmax(x, axis=axis)

def _gelu(x):
    return jax.nn.gelu(x, approximate=True)

def _silu(x):
    return jax.nn.silu(x)

def _sigmoid(x):
    return jax.nn.sigmoid(x)

def _layernorm(x, axis=-1, eps=1e-05):
    m = jnp.mean(x, axis=axis, keepdims=True)
    v = jnp.var(x, axis=axis, keepdims=True)
    return (x - m) / jnp.sqrt(v + eps)

def _scatter_add(tgt, idx, src, axis=0):
    return tgt.at[idx].add(src)

def _segment_sum(src, seg, n):
    return jax.ops.segment_sum(src, seg, n)
kernel_name = 'mk_xattn_ffn_d1_seqx_r8_deec02'

def setup_inputs(seed: int=0):
    np.random.seed(seed)
    _w = jnp.asarray

    def _rec_inputs():
        import jax
        import jax.numpy as jnp
        _rk = jax.random.key(seed)
        x = -0.0002928 + 1 * jax.random.normal(jax.random.fold_in(_rk, 1), (16, 64, 256), jnp.float32)
        _lenS = 64 - jax.random.randint(jax.random.fold_in(_rk, 7), (16,), 0, max(1, 64 // 4) + 1, jnp.int32)
        _lenS2 = 64 - jax.random.randint(jax.random.fold_in(_rk, 8), (16,), 0, max(1, 64 // 4) + 1, jnp.int32)
        _ctx_512P = jax.random.normal(jax.random.fold_in(_rk, 11), (16, 16, 64), jnp.float32)
        _ctx_512c = jax.random.dirichlet(jax.random.fold_in(_rk, 511), 0.3 * jnp.ones((16,), jnp.float32), (16, 64))
        _ctx_512t = jnp.einsum('bsk,bkd->bsd', _ctx_512c, _ctx_512P)
        _ctx_512t = _ctx_512t * jax.lax.rsqrt(jnp.mean(jnp.square(_ctx_512t)) + 1e-12) * 0.953939
        ctx_512 = 0.000227908 + 0.99994 * (_ctx_512t + 0.3 * jax.random.normal(jax.random.fold_in(_rk, 611), (16, 64, 64), jnp.float32))
        return (x, ctx_512)
    x, ctx_512 = _rec_inputs()

    def _L0_xattn_setup():
        import jax, jax.numpy as jnp
        import numpy as np
        B, S, L = (2, 128, 128)
        DIM_Q, H, K, D_C, D_CQ, R = (256, 16, 128, 64, 192, 64)

        def _rope_tables(seq_len, dim, dtype):
            inv_freq = 1.0 / 10000.0 ** (jnp.arange(0, dim, 2, dtype=dtype) / dim)
            t = jnp.arange(seq_len, dtype=dtype)
            freqs = t[:, None] * inv_freq[None, :]
            sin = jnp.repeat(jnp.sin(freqs), 2, axis=-1)
            cos = jnp.repeat(jnp.cos(freqs), 2, axis=-1)
            return (sin, cos)

        def _rotate_half(x):
            h = x.shape[-1] // 2
            return jnp.concatenate([-x[..., h:], x[..., :h]], axis=-1)
        key = jax.random.key(seed)
        ks = jax.random.split(key, 8)
        s_in = 1.0 / np.sqrt(DIM_Q)
        s_k = 1.0 / np.sqrt(K)
        s_cq = 1.0 / np.sqrt(D_CQ)
        s_c = 1.0 / np.sqrt(D_C)
        return {'hidden_q': jax.random.normal(ks[0], (B, S, DIM_Q), jnp.float32), 'kv_c': jax.random.normal(ks[1], (B, L, D_C), jnp.float32), 'Wq': jax.random.normal(ks[2], (H * K, DIM_Q), jnp.float32) * s_in, 'w_kc_q': jax.random.normal(ks[3], (H, K, D_CQ), jnp.float32) * s_k, 'w_kc_kv': jax.random.normal(ks[4], (H, K, D_C), jnp.float32) * s_k, 'W_qr': jax.random.normal(ks[5], (H, D_CQ, R), jnp.float32) * s_cq / np.sqrt(R), 'W_kr': jax.random.normal(ks[6], (H, D_C, R), jnp.float32) * s_c, 'Wo': jax.random.normal(ks[7], (DIM_Q, H * K), jnp.float32) * s_k}
    _L0_xattn_all = _L0_xattn_setup()
    _L0_xattn_in = {k: v for k, v in _L0_xattn_all.items() if k in ('Wq', 'w_kc_q', 'w_kc_kv', 'W_qr', 'W_kr', 'Wo')}
    del _L0_xattn_all

    def _L0_ffn_setup():
        import jax, jax.numpy as jnp
        import numpy as np
        TOP_K = 4
        NUM_EXPERTS = 16
        key = jax.random.key(seed)
        ks = jax.random.split(key, 6)
        B, S, H, I, E = (2, 128, 256, 224, NUM_EXPERTS)
        return {'x': jax.random.normal(ks[0], (B, S, H), dtype=jnp.float32), 'router_w': jax.random.normal(ks[1], (E, H), dtype=jnp.float32) * 0.02, 'expert_bias': jnp.zeros((E,), dtype=jnp.float32), 'gate_proj': jax.random.normal(ks[2], (E, H, I), dtype=jnp.float32) * 0.02, 'up_proj': jax.random.normal(ks[3], (E, H, I), dtype=jnp.float32) * 0.02, 'down_proj': jax.random.normal(ks[4], (E, I, H), dtype=jnp.float32) * 0.02}
    _L0_ffn_all = _L0_ffn_setup()
    _L0_ffn_in = {k: v for k, v in _L0_ffn_all.items() if k in ('router_w', 'expert_bias', 'gate_proj', 'up_proj', 'down_proj')}
    del _L0_ffn_all
    return {'x': x, 'ctx_512': ctx_512, 'L0_xattn_Wq': _L0_xattn_in['Wq'], 'L0_xattn_w_kc_q': _L0_xattn_in['w_kc_q'], 'L0_xattn_w_kc_kv': _L0_xattn_in['w_kc_kv'], 'L0_xattn_W_qr': _L0_xattn_in['W_qr'], 'L0_xattn_W_kr': _L0_xattn_in['W_kr'], 'L0_xattn_Wo': _L0_xattn_in['Wo'], 'L0_ffn_router_w': _L0_ffn_in['router_w'], 'L0_ffn_expert_bias': _L0_ffn_in['expert_bias'], 'L0_ffn_gate_proj': _L0_ffn_in['gate_proj'], 'L0_ffn_up_proj': _L0_ffn_in['up_proj'], 'L0_ffn_down_proj': _L0_ffn_in['down_proj']}

def reference(x, ctx_512, L0_xattn_Wq, L0_xattn_w_kc_q, L0_xattn_w_kc_kv, L0_xattn_W_qr, L0_xattn_W_kr, L0_xattn_Wo, L0_ffn_router_w, L0_ffn_expert_bias, L0_ffn_gate_proj, L0_ffn_up_proj, L0_ffn_down_proj):
    import jax
    import jax.numpy as jnp

    def _L0_xattn_ref(hidden_q, kv_c, Wq, w_kc_q, w_kc_kv, W_qr, W_kr, Wo):
        import jax, jax.numpy as jnp
        import numpy as np
        B, S, L = (2, 128, 128)
        DIM_Q, H, K, D_C, D_CQ, R = (256, 16, 128, 64, 192, 64)

        def _rope_tables(seq_len, dim, dtype):
            inv_freq = 1.0 / 10000.0 ** (jnp.arange(0, dim, 2, dtype=dtype) / dim)
            t = jnp.arange(seq_len, dtype=dtype)
            freqs = t[:, None] * inv_freq[None, :]
            sin = jnp.repeat(jnp.sin(freqs), 2, axis=-1)
            cos = jnp.repeat(jnp.cos(freqs), 2, axis=-1)
            return (sin, cos)

        def _rotate_half(x):
            h = x.shape[-1] // 2
            return jnp.concatenate([-x[..., h:], x[..., :h]], axis=-1)
        b, s, _ = hidden_q.shape
        l = kv_c.shape[1]
        q_hk = (hidden_q @ Wq.T).reshape(b, s, H, K)
        q_big = jnp.einsum('bshk,hkq->bshq', q_hk, w_kc_q)
        sin, cos = _rope_tables(l, D_C, kv_c.dtype)
        kv_rope = kv_c * cos[None] + _rotate_half(kv_c) * sin[None]
        q_r = jnp.einsum('bshq,hqr->bhsr', q_big, W_qr)
        k_r = jnp.einsum('bld,hdr->bhlr', kv_rope, W_kr)
        scores = jnp.einsum('bhsr,bhlr->bhsl', q_r, k_r)
        attn = jax.nn.softmax(scores, axis=-1)
        ctx_c = jnp.einsum('bhsl,bld->bhsd', attn, kv_rope)
        ctx_lat = jnp.einsum('bhsd,hkd->bshk', ctx_c, w_kc_kv)
        out = ctx_lat.reshape(b, s, H * K) @ Wo.T
        return out

    def _L0_ffn_ref(x, router_w, expert_bias, gate_proj, up_proj, down_proj):
        import jax, jax.numpy as jnp
        import numpy as np
        TOP_K = 4
        NUM_EXPERTS = 16
        logits = jnp.einsum('bsh,eh->bse', x, router_w) + expert_bias
        scores = jax.nn.softmax(logits, axis=-1)
        top_w, top_idx = jax.lax.top_k(scores, TOP_K)
        top_w = top_w / jnp.sum(top_w, axis=-1, keepdims=True)
        g = jnp.einsum('bsh,khe->bske', x, gate_proj)
        u = jnp.einsum('bsh,khe->bske', x, up_proj)
        act = jax.nn.silu(g) * u
        out = jnp.einsum('bske,keh->bskh', act, down_proj)
        sel = jnp.take_along_axis(out, top_idx[..., None], axis=2)
        return jnp.sum(sel * top_w[..., None], axis=2)
    x = x + _L0_xattn_ref(_layernorm(x, axis=-1), ctx_512, L0_xattn_Wq, L0_xattn_w_kc_q, L0_xattn_w_kc_kv, L0_xattn_W_qr, L0_xattn_W_kr, L0_xattn_Wo)
    x = x + _L0_ffn_ref(_layernorm(x, axis=-1), L0_ffn_router_w, L0_ffn_expert_bias, L0_ffn_gate_proj, L0_ffn_up_proj, L0_ffn_down_proj)
    return x

_drawn_inputs = setup_inputs


def setup_inputs(seed=0):
    import zlib

    import numpy as np

    out = dict(_drawn_inputs(seed))
    spreads = {'L0_ffn_expert_bias': (0.0, 0.8)}
    factors = {'L0_ffn_router_w': 8.0,
     'L0_ffn_gate_proj': 8.0,
     'L0_ffn_up_proj': 8.0,
     'L0_ffn_down_proj': 8.0}
    for name, (base, spread) in spreads.items():
        noise = np.random.default_rng([zlib.crc32(name.encode()), seed]).standard_normal(out[name].shape)
        drawn = base * np.exp(spread * noise) if base else spread * noise
        out[name] = jnp.asarray(drawn.astype(out[name].dtype))
    for name, factor in factors.items():
        out[name] = (out[name] * factor).astype(out[name].dtype)
    return out
```

```python
from contextlib import ExitStack

import numpy as np

import concourse.bass as bass
from concourse import mybir

F32 = mybir.dt.float32
U32 = mybir.dt.uint32
ALU = mybir.AluOpType
ACT = mybir.ActivationFunctionType
AX = mybir.AxisListType

P = 128
B, S, D = 16, 64, 256
L, DC = 64, 64
H, K, CQ, R = 16, 128, 192, 64
E, F, TOPK = 16, 224, 4
T = B * S // P
IC = D // P
FH = F // 2
NP = H // 2
EPS = 1e-5


def build(nc, x, ctxd, rope_c, rope_s, wqrT, wkrT, kcqT_a, kcqT_b, wq, kckv, woT,
          rwT, bias, wgu, wd, ident, half, iota, out):
    with ExitStack() as es:
        def sb(name, shape, dt=F32):
            return es.enter_context(nc.sbuf_tensor(name, shape, dt))

        def sem(name):
            return es.enter_context(nc.semaphore(name))

        X = sb("X", [P, T, D])
        XN = sb("XN", [P, T, D])
        XNT = sb("XNT", [P, IC, T * P])
        KVD = sb("KVD", [P, B, DC])
        RC = sb("RC", [P, DC])
        RS = sb("RS", [P, DC])
        HALF = sb("HALF", [P, 2])
        KR = sb("KR", [P, B, DC])
        KT1 = sb("KT1", [P, B, DC])
        KVT = sb("KVT", [P, B, L])
        BD = sb("BD", [P, 2, P])
        WQR = sb("WQR", [R, H, CQ])
        WKR = sb("WKR", [R, H, DC])
        WORK = sb("WORK", [P, 2 * H * K])
        KCA = WORK[:, 0:H * K].rearrange("p (h k) -> p h k", h=H)
        KCB = WORK[0:CQ - P, H * K:].rearrange("p (h k) -> p h k", h=H)
        STAGE = sb("STAGE", [P, 2 * H * D])
        WQ = STAGE[:, 0:H * D].rearrange("p (h i) -> p h i", h=H)
        WO = STAGE[:, H * D:].rearrange("p (h i) -> p h i", h=H)
        WD = STAGE[0:FH, :].rearrange("p (e c i) -> p e c i", e=E, c=2)
        KCKV = sb("KCKV", [P, H, DC])
        CA = sb("CA", [P, H, DC])
        CB = sb("CB", [CQ - P, H, DC])
        EK = sb("EK", [P, H, DC])
        M = sb("M", [P, IC, H, DC])
        N = sb("N", [P, NP, D])
        GD = sb("GD", [P, NP, 2, P])
        PR = WORK[:, 0:1024].rearrange("p (b q l) -> p b q l", b=2, q=NP)
        PT = WORK[:, 1024:2048].rearrange("p (b n) -> p b n", b=2)
        CT = WORK[:, 2048:3072].rearrange("p (q n) -> p q n", q=NP)
        MX = sb("MX", [P, 2, NP])
        SM = sb("SM", [P, 2, NP])
        RI = sb("RI", [P, 2, NP])
        ST6 = sb("ST6", [P, T, 6])
        MV = sb("MV", [P, T, 2])
        VE = sb("VE", [P, T])
        RSTD = sb("RSTD", [P, T])
        ST62 = sb("ST62", [P, 6])
        MV2 = sb("MV2", [P, 2])
        VE2 = sb("VE2", [P, 1])
        RSTD2 = sb("RSTD2", [P, 1])
        MH = sb("MH", [P, 1])
        XN2 = sb("XN2", [P, D])
        XN2T = XN[:, :, :].rearrange("p t i -> p (t i)").rearrange("p (c n) -> p c n", c=IC)
        XN2C = sb("XN2C", [P, IC, P])
        RW = sb("RW", [P, IC, E])
        BI = sb("BI", [P, E])
        IDN = sb("IDN", [P, P])
        IOTA = sb("IOTA", [P, E])
        LG = sb("LG", [P, E])
        M8 = sb("M8", [P, 8])
        I8 = sb("I8", [P, 8], U32)
        I4F = sb("I4F", [P, TOPK])
        D4 = sb("D4", [P, TOPK])
        W4 = sb("W4", [P, TOPK])
        S4 = sb("S4", [P, 1])
        R4 = sb("R4", [P, 1])
        OH = sb("OH", [P, E, TOPK])
        OW = sb("OW", [P, E, TOPK])
        WT = sb("WT", [P, T, E])
        WGU = sb("WGU", [P, E, IC, 2 * F])
        SG = WORK[:, 3072:3072 + 2 * F].rearrange("p (b f) -> p b f", b=2)
        AC = WORK[:, 3584:3584 + 2 * F].rearrange("p (b f) -> p b f", b=2)
        ACT_T = CA[0:FH, :, :].rearrange("p h d -> p (h d)")[:, 0:4 * P].rearrange("p (b c n) -> p b c n", b=2, c=2)
        bank = [es.enter_context(nc.psum_tensor(f"bank{i}", [P, 512], F32)) for i in range(8)]

        ld = {n: sem(f"ld_{n}") for n in ("x", "kv", "const", "qr", "kc0", "kc1", "wq0", "wq1", "kckv", "wo0", "wo1",
                                          "router", "wgu", "wd")}
        absorb_done = sem("absorb_done")
        setup = sem("setup")
        ln_stats, ln_aggr, ln_eps, ln_rstd, ln_done = (sem(n) for n in ("ln_stats", "ln_aggr", "ln_eps", "ln_rstd", "ln_done"))
        ropa, ropb, ropc = sem("rope_cos"), sem("rope_sin"), sem("rope_done")
        xt_done, xt_evac = sem("xt_done"), sem("xt_evac")
        kvt_done, kvt_evac = sem("kvt_done"), sem("kvt_evac")
        c_done, c_evac = sem("c_done"), sem("c_evac")
        ek_done, ek_evac = sem("ek_done"), sem("ek_evac")
        m_done, m_evac = sem("m_done"), sem("m_evac")
        n_done, n_evac = sem("n_done"), sem("n_evac")
        g_done, g_evac_a, g_evac_v = sem("g_done"), sem("g_evac_act"), sem("g_evac_dve")
        s_done, max_done, sub_done, exp_done = sem("s_done"), sem("max_done"), sem("sub_done"), sem("exp_done")
        sum_done, rcp_done, norm_done = sem("sum_done"), sem("rcp_done"), sem("norm_done")
        pt_done, pt_evac = sem("pt_done"), sem("pt_evac")
        bd_ready = sem("bd_ready")
        ctx_done, ctx_evac = sem("ctx_done"), sem("ctx_evac")
        out_done, x1_done = sem("out_done"), sem("x1_done")
        l2_stats, l2_aggr, l2_eps, l2_rstd, l2_done = (sem(n) for n in ("l2_stats", "l2_aggr", "l2_eps", "l2_rstd", "l2_done"))
        xt2_done, xt2_evac, xt2_kept = sem("xt2_done"), sem("xt2_evac"), sem("xt2_kept")
        lg_done, lg_read, rt = sem("lg_done"), sem("lg_read"), sem("router_step")
        top_exp, xtra, wt_done = sem("top_exp"), sem("weights_step"), sem("weights_done")
        gu_done, silu_done, act_done = sem("gu_done"), sem("silu_done"), sem("act_done")
        at_done, at_evac = sem("at_done"), sem("at_evac")
        y_done, y_added = sem("y_done"), sem("y_added")
        stored = sem("stored")

        block = es.enter_context(nc.Block())

        @block.sync
        def _(sp):
            sp.dma_start(X[:, :, :], x).then_inc(ld["x"], 16)
            sp.dma_start(KVD[:, :, :], ctxd).then_inc(ld["kv"], 16)
            for dst, src in ((RC, rope_c), (RS, rope_s), (IDN, ident), (HALF, half)):
                sp.dma_start(dst[:, :], src).then_inc(ld["const"], 16)
            sp.dma_start(WQR[:, :, :], wqrT).then_inc(ld["qr"], 16)
            sp.dma_start(WKR[:, :, :], wkrT).then_inc(ld["qr"], 16)
            for g in range(2):
                h = slice(8 * g, 8 * g + 8)
                sp.dma_start(KCA[:, h, :], kcqT_a[:, h, :]).then_inc(ld[f"kc{g}"], 16)
                sp.dma_start(KCB[:, h, :], kcqT_b[:, h, :]).then_inc(ld[f"kc{g}"], 16)
            for g in range(2):
                sp.dma_start(WQ[:, 8 * g:8 * g + 8, :], wq[:, 8 * g:8 * g + 8, :]).then_inc(ld[f"wq{g}"], 16)
            sp.dma_start(KCKV[:, :, :], kckv).then_inc(ld["kckv"], 16)
            for g in range(2):
                sp.dma_start(WO[:, 8 * g:8 * g + 8, :], woT[:, 8 * g:8 * g + 8, :]).then_inc(ld[f"wo{g}"], 16)
            for dst, src in ((RW, rwT),):
                sp.dma_start(dst[:, :, :], src).then_inc(ld["router"], 16)
            for dst, src in ((BI, bias), (IOTA, iota)):
                sp.dma_start(dst[:, :], src).then_inc(ld["router"], 16)
            sp.dma_start(WGU[:, :, :, :], wgu).then_inc(ld["wgu"], 16)
            sp.wait_ge(m_done, 4)
            sp.wait_ge(n_done, 4)
            sp.dma_start(WD, wd).then_inc(ld["wd"], 16)
            sp.wait_ge(y_added, E * T)
            sp.dma_start(out, X[:, :, :]).then_inc(stored, 16)
            sp.wait_ge(stored, 16)

        @block.gpsimd
        def _(gp):
            gp.memset(MH[:, :], -0.5).then_inc(setup, 1)
            gp.memset(GD[:, :, :, :], 0.0).then_inc(setup, 1)
            gp.wait_ge(ld["kv"], 16)
            gp.wait_ge(ld["const"], 64)
            hd = DC // 2
            for lo in (0, hd):
                src = hd - lo
                gp.tensor_tensor(KT1[:, :, lo:lo + hd], KVD[:, :, src:src + hd],
                                 RS[:, lo:lo + hd].unsqueeze(1).to_broadcast([P, B, hd]), ALU.mult).then_inc(ropa, 1)
            gp.tensor_tensor(KR[:, :, :], KVD[:, :, :], RC[:, :].unsqueeze(1).to_broadcast([P, B, DC]),
                             ALU.mult).then_inc(ropa, 1)
            gp.wait_ge(ropa, 3)
            gp.tensor_tensor(KR[:, :, :], KR[:, :, :], KT1[:, :, :], ALU.add).then_inc(ropc, 1)
            gp.wait_ge(setup, 2)
            gp.wait_ge(ln_eps, 1)
            gp.tensor_tensor(RSTD[:, :], VE[:, :], MH[:, :].to_broadcast([P, T]), ALU.pow).then_inc(ln_rstd, 1)
            gp.wait_ge(ropc, 1)

            def tile(t, first=False):
                if not first:
                    gp.wait_ge(ctx_done, 2 * t)
                gp.tensor_tensor(BD[:, :, :].rearrange("p b (c d) -> p b c d", c=2),
                                 KR[:, bass.ds(2 * t, 2), :].unsqueeze(2).to_broadcast([P, 2, 2, DC]),
                                 HALF[:, :].unsqueeze(1).unsqueeze(3).to_broadcast([P, 2, 2, DC]),
                                 ALU.mult).then_inc(bd_ready, 1)

            def keep(t):
                gp.wait_ge(xt2_evac, t + 1)
                gp.tensor_copy(XN2T[:, :, bass.ts(t, P)], XN2C[:, :, :]).then_inc(xt2_kept, 1)

            def rstd2(t):
                gp.wait_ge(l2_eps, t + 1)
                gp.tensor_tensor(RSTD2[:, :], VE2[:, :], MH[:, :], ALU.pow).then_inc(l2_rstd, 1)

            tile(0, first=True)
            with gp.Fori(1, T) as t:
                tile(t)
                rstd2(t - 1)
                keep(t - 1)
            rstd2(T - 1)
            keep(T - 1)

        @block.scalar
        def _(act):
            def evac(dst, src):
                return act.activation(dst, src, ACT.Copy)
            for q in range(4):
                act.wait_ge(xt_done, q + 1)
                evac(XNT[:, :, 2 * q * P:(2 * q + 2) * P],
                     bank[q][:, :].rearrange("p (c n) -> p c n", c=IC)).then_inc(xt_evac, 1)
            for q in range(2):
                act.wait_ge(kvt_done, q + 1)
                evac(KVT[:, 8 * q:8 * q + 8, :],
                     bank[4 + q][:, :].rearrange("p (b l) -> p b l", b=8)).then_inc(kvt_evac, 1)
            for g in range(2):
                h = slice(8 * g, 8 * g + 8)
                act.wait_ge(c_done, g + 1)
                evac(CA[:, h, :], bank[g][:, :].rearrange("p (h d) -> p h d", h=8)).then_inc(c_evac, 1)
                evac(CB[:, h, :], bank[2 + g][0:CQ - P, :].rearrange("p (h d) -> p h d", h=8)).then_inc(c_evac, 1)
            for g in range(2):
                act.wait_ge(ek_done, g + 1)
                evac(EK[:, 8 * g:8 * g + 8, :],
                     bank[4 + g][:, :].rearrange("p (h d) -> p h d", h=8)).then_inc(ek_evac, 1)
            for g in range(4):
                act.wait_ge(m_done, g + 1)
                evac(M[:, :, 4 * g:4 * g + 4, :],
                     bank[6 + g % 2][:, :].rearrange("p (c h d) -> p c h d", c=IC, h=4)).then_inc(m_evac, 1)
            for j in range(4):
                act.wait_ge(n_done, j + 1)
                evac(N[:, 2 * j:2 * j + 2, :], bank[j][:, :].rearrange("p (h o) -> p h o", h=2)).then_inc(n_evac, 1)
            act.wait_ge(setup, 2)

            def g_half(t, g, first=False):
                act.wait_ge(g_done, 2 * t + g + 1)
                if not first:
                    act.wait_ge(s_done, 2 * t)
                evac(GD[0:64, 4 * g:4 * g + 4, :, 0:64],
                     bank[g][0:64, :].rearrange("p (q b s) -> p q b s", q=4, b=2)).then_inc(g_evac_a, 1)

            def exp(t, b):
                act.wait_ge(sub_done, 2 * t + b + 1)
                act.activation(PR[:, b, :, :], PR[:, b, :, :], ACT.Exp).then_inc(exp_done, 1)

            def pt(t, b, first=False):
                act.wait_ge(pt_done, 2 * t + b + 1)
                if not first:
                    act.wait_ge(ctx_done, 2 * t + b - 1)
                evac(PT[:, b, :], bank[2 + b][:, :]).then_inc(pt_evac, 1)

            def xt2(t, first=False):
                act.wait_ge(xt2_done, t + 1)
                if not first:
                    act.wait_ge(xt2_kept, t)
                    act.wait_ge(lg_done, t)
                evac(XN2C[:, :, :], bank[6][:, 0:IC * P].rearrange("p (c n) -> p c n", c=IC)).then_inc(xt2_evac, 1)

            def top(t):
                act.wait_ge(rt, 6 * t + 2)
                act.activation(D4[:, :], D4[:, :], ACT.Exp, accum_out=S4[:, :]).then_inc(top_exp, 1)

            def tile(t, first=False, second=False, last=False):
                exp(t, 0)
                exp(t, 1)
                pt(t, 0, first)
                if not last:
                    g_half(t + 1, 0)
                pt(t, 1, first)
                if not last:
                    g_half(t + 1, 1)
                if not first:
                    xt2(t - 1, second)
                    top(t - 1)

            g_half(0, 0, True)
            g_half(0, 1, True)
            tile(0, first=True)
            tile(1, second=True)
            with act.Fori(2, T - 1) as t:
                tile(t)
            tile(T - 1, last=True)
            xt2(T - 1)
            top(T - 1)

            def expert(e, first=False):
                for t in range(T + 1):
                    if t < T:
                        act.wait_ge(gu_done, T * e + t + 1)
                        if not first or t >= 2:
                            act.wait_ge(act_done, T * e + t - 1)
                        act.activation(SG[:, t % 2, :], bank[t % 2][:, 0:F], ACT.Silu).then_inc(silu_done, 1)
                    if t > 0:
                        u = t - 1
                        act.wait_ge(at_done, T * e + u + 1)
                        if not first or u >= 2:
                            act.wait_ge(y_done, T * e + u - 1)
                        evac(ACT_T[:, u % 2, :, :],
                             bank[2 + u % 2][0:FH, 0:2 * P].rearrange("p (c n) -> p c n", c=2)).then_inc(at_evac, 1)

            expert(0, True)
            with act.Fori(1, E) as e:
                expert(e)

        @block.vector
        def _(dve):
            dve.wait_ge(ld["x"], 16)
            for t in range(T):
                dve.bn_stats(ST6[:, t, :], X[:, t, :]).then_inc(ln_stats, 1)
            for t in range(T):
                dve.wait_ge(ln_stats, t + 1)
                dve.bn_aggr(MV[:, t, :], ST6[:, t, :]).then_inc(ln_aggr, 1)
            dve.wait_ge(ln_aggr, T)
            dve.tensor_scalar(VE[:, :], MV[:, :, 1], EPS, None, ALU.add).then_inc(ln_eps, 1)
            dve.wait_ge(ln_rstd, 1)
            for t in range(T):
                dve.tensor_scalar(XN[:, t, :], X[:, t, :], MV[:, t, 0:1], RSTD[:, t:t + 1],
                                  ALU.subtract, ALU.mult).then_inc(ln_done, 1)
            dve.wait_ge(setup, 2)

            def g_half(t, g, first=False):
                dve.wait_ge(g_done, 2 * t + g + 1)
                if not first:
                    dve.wait_ge(s_done, 2 * t)
                dve.tensor_copy(GD[64:128, 4 * g:4 * g + 4, :, 64:128],
                                bank[g][64:128, :].rearrange("p (q b s) -> p q b s", q=4, b=2)).then_inc(g_evac_v, 1)

            def scores(t, b, first=False):
                u = 2 * t + b
                sc = bank[2 + b][:, :].rearrange("p (q l) -> p q l", q=NP)
                dve.wait_ge(s_done, u + 1)
                dve.tensor_reduce(MX[:, b, :], sc, AX.X, ALU.max).then_inc(max_done, 1)
                dve.wait_ge(max_done, u + 1)
                if not first:
                    dve.wait_ge(pt_done, u - 1)
                dve.tensor_tensor(PR[:, b, :, :], sc, MX[:, b, :].unsqueeze(2).to_broadcast([P, NP, L]),
                                  ALU.subtract).then_inc(sub_done, 1)

            def norm(t, b):
                u = 2 * t + b
                dve.wait_ge(exp_done, u + 1)
                dve.tensor_reduce(SM[:, b, :], PR[:, b, :, :], AX.X, ALU.add).then_inc(sum_done, 1)
                dve.wait_ge(sum_done, u + 1)
                dve.reciprocal(RI[:, b, :], SM[:, b, :]).then_inc(rcp_done, 1)
                dve.wait_ge(rcp_done, u + 1)
                dve.tensor_tensor(PR[:, b, :, :], PR[:, b, :, :], RI[:, b, :].unsqueeze(2).to_broadcast([P, NP, L]),
                                  ALU.mult).then_inc(norm_done, 1)

            def latent(t, b, first=False):
                dve.wait_ge(ctx_done, 2 * t + b + 1)
                if not first:
                    dve.wait_ge(out_done, t)
                dve.tensor_copy(CT[:, :, 64 * b:64 * b + 64],
                                bank[4][:, :].rearrange("p (q s) -> p q s", q=NP)).then_inc(ctx_evac, 1)

            def wait_alone(s, n):
                dve.wait_ge(setup, 2)
                dve.wait_ge(s, n)

            def residual(t):
                dve.wait_ge(out_done, t + 1)
                xt = X[:, bass.ds(t, 1), :].rearrange("p a i -> p (a i)")
                dve.tensor_tensor(xt, bank[5][:, 0:D], xt, ALU.add).then_inc(x1_done, 1)
                wait_alone(x1_done, t + 1)
                dve.bn_stats(ST62[:, :], xt).then_inc(l2_stats, 1)
                wait_alone(l2_stats, t + 1)
                dve.bn_aggr(MV2[:, :], ST62[:, :]).then_inc(l2_aggr, 1)
                dve.wait_ge(l2_aggr, t + 1)
                dve.tensor_scalar(VE2[:, :], MV2[:, 1:2], EPS, None, ALU.add).then_inc(l2_eps, 1)

            def norm2(t, first=False):
                dve.wait_ge(l2_rstd, t + 1)
                if not first:
                    dve.wait_ge(xt2_done, t)
                xt = X[:, bass.ds(t, 1), :].rearrange("p a i -> p (a i)")
                dve.tensor_scalar(XN2[:, :], xt, MV2[:, 0:1], RSTD2[:, :], ALU.subtract, ALU.mult).then_inc(l2_done, 1)

            def router(t):
                r = 6 * t
                dve.wait_ge(lg_done, t + 1)
                dve.tensor_tensor(LG[:, :], bank[7][:, 0:E], BI[:, :], ALU.add).then_inc(lg_read, 1)
                wait_alone(lg_read, t + 1)
                dve.max(M8[:, :], LG[:, :]).then_inc(rt, 1)
                dve.wait_ge(rt, r + 1)
                dve.tensor_scalar(D4[:, :], M8[:, 0:TOPK], M8[:, 0:1], None, ALU.subtract).then_inc(rt, 1)
                dve.max_index(I8[:, :], M8[:, :], LG[:, :]).then_inc(rt, 1)
                dve.wait_ge(rt, r + 3)
                dve.tensor_copy(I4F[:, :], I8[:, 0:TOPK]).then_inc(rt, 1)
                dve.wait_ge(rt, r + 4)
                dve.tensor_tensor(OH[:, :, :], IOTA[:, :].unsqueeze(2).to_broadcast([P, E, TOPK]),
                                  I4F[:, :].unsqueeze(1).to_broadcast([P, E, TOPK]), ALU.is_equal).then_inc(rt, 1)
                dve.wait_ge(top_exp, t + 1)
                dve.reciprocal(R4[:, :], S4[:, :]).then_inc(rt, 1)
                dve.wait_ge(rt, r + 6)
                dve.tensor_scalar(W4[:, :], D4[:, :], R4[:, :], None, ALU.mult).then_inc(xtra, 1)
                dve.wait_ge(xtra, 2 * t + 1)
                dve.tensor_tensor(OW[:, :, :], OH[:, :, :], W4[:, :].unsqueeze(1).to_broadcast([P, E, TOPK]),
                                  ALU.mult).then_inc(xtra, 1)
                dve.wait_ge(xtra, 2 * t + 2)
                dve.tensor_reduce(WT[:, bass.ds(t, 1), :].rearrange("p a e -> p (a e)"), OW[:, :, :], AX.X,
                                  ALU.add).then_inc(wt_done, 1)
                dve.wait_ge(wt_done, t + 1)

            def tile(t, first=False, second=False, last=False):
                scores(t, 0, first)
                scores(t, 1, first)
                if not first:
                    residual(t - 1)
                norm(t, 0)
                norm(t, 1)
                if not first:
                    norm2(t - 1, second)
                if not last:
                    g_half(t + 1, 0)
                latent(t, 0, first)
                if not last:
                    g_half(t + 1, 1)
                if not first:
                    router(t - 1)
                latent(t, 1, first)

            dve.wait_ge(ld["router"], 48)
            g_half(0, 0, True)
            g_half(0, 1, True)
            tile(0, first=True)
            tile(1, second=True)
            with dve.Fori(2, T - 1) as t:
                tile(t)
            tile(T - 1, last=True)
            residual(T - 1)
            norm2(T - 1)
            router(T - 1)

            def expert(e, first=False):
                for t in range(T + 2):
                    if t < T:
                        dve.wait_ge(silu_done, T * e + t + 1)
                        if not first or t >= 2:
                            dve.wait_ge(at_done, T * e + t - 1)
                        dve.tensor_tensor(AC[:, t % 2, :], SG[:, t % 2, :], bank[t % 2][:, F:2 * F], ALU.mult).then_inc(act_done, 1)
                    if t > 1:
                        u = t - 2
                        dve.wait_ge(y_done, T * e + u + 1)
                        if not first:
                            dve.wait_ge(y_added, T * (e - 1) + u + 1)
                        dve.scalar_tensor_tensor(X[:, u, :], bank[4 + u % 2][:, 0:D],
                                                 WT[:, u, bass.ds(e, 1)] if not first else WT[:, u, 0:1],
                                                 X[:, u, :], ALU.mult, ALU.add).then_inc(y_added, 1)

            expert(0, True)
            with dve.Fori(1, E) as e:
                expert(e)

        @block.tensor
        def _(pe):
            pe.wait_ge(ld["const"], 64)
            for t in range(T):
                pe.wait_ge(ln_done, t + 1)
                for c in range(IC):
                    last = pe.transpose(bank[t // 2][:, c * 2 * P + (t % 2) * P:c * 2 * P + (t % 2 + 1) * P],
                                        XN[:, t, c * P:(c + 1) * P], IDN[:, :])
                if t % 2:
                    last.then_inc(xt_done, 1)
            pe.wait_ge(ld["qr"], 32)
            for g in range(2):
                pe.wait_ge(xt_evac, 4)
                for h in range(8 * g, 8 * g + 8):
                    o = slice((h % 8) * DC, (h % 8 + 1) * DC)
                    pe.matmul(bank[g][:, o], WQR[:, h, 0:P], WKR[:, h, :], start=True, stop=True)
                    last = pe.matmul(bank[2 + g][0:CQ - P, o], WQR[:, h, P:CQ], WKR[:, h, :], start=True, stop=True)
                last.then_inc(c_done, 1)
            pe.wait_ge(ropc, 1)
            for b in range(B):
                last = pe.matmul(bank[4 + b // 8][0:64, (b % 8) * L:(b % 8 + 1) * L], KR[0:64, b, :], IDN[0:64, 0:64],
                                 start=True, stop=True)
                last = pe.matmul(bank[4 + b // 8][64:128, (b % 8) * L:(b % 8 + 1) * L], KR[64:128, b, :],
                                 IDN[64:128, 64:128], start=True, stop=True)
                if b % 8 == 7:
                    last.then_inc(kvt_done, 1)
            for g in range(2):
                pe.wait_ge(ld[f"kc{g}"], 32)
                pe.wait_ge(c_evac, 2 * g + 2)
                pe.wait_ge(kvt_evac, g + 1)
                for h in range(8 * g, 8 * g + 8):
                    o = bank[4 + g][:, (h % 8) * DC:(h % 8 + 1) * DC]
                    pe.matmul(o, KCA[:, h, :], CA[:, h, :], start=True, stop=False)
                    last = pe.matmul(o, KCB[:, h, :], CB[:, h, :], start=False, stop=True)
                last.then_inc(ek_done, 1)
            for g in range(4):
                pe.wait_ge(ld[f"wq{g // 2}"], 16)
                pe.wait_ge(ek_evac, g // 2 + 1)
                if g >= 2:
                    pe.wait_ge(m_evac, g - 1)
                for h in range(4 * g, 4 * g + 4):
                    for c in range(IC):
                        o = (c * 4 + h % 4) * DC
                        last = pe.matmul(bank[6 + g % 2][:, o:o + DC], WQ[:, h, c * P:(c + 1) * P], EK[:, h, :],
                                         start=True, stop=True)
                last.then_inc(m_done, 1)
            pe.wait_ge(ld["kckv"], 16)
            for j in range(4):
                pe.wait_ge(ld[f"wo{j // 2}"], 16)
                pe.wait_ge(c_evac, 4)
                for p2 in range(2):
                    for h2 in range(2):
                        h = 4 * j + 2 * p2 + h2
                        last = pe.matmul(bank[j][64 * p2:64 * p2 + 64, h2 * D:(h2 + 1) * D], KCKV[:, h, :], WO[:, h, :],
                                         start=True, stop=True)
                last.then_inc(n_done, 1)

            def queries(t, g, first=False):
                if not first:
                    pe.wait_ge(g_evac_a, 2 * t + g - 1)
                    pe.wait_ge(g_evac_v, 2 * t + g - 1)
                for q in range(4):
                    for c in range(IC):
                        h = 8 * g + 2 * q
                        last = pe.matmul(bank[g][:, q * P:(q + 1) * P],
                                         M[:, c, h:h + 2, :].rearrange("p h d -> p (h d)"),
                                         XNT[:, c, bass.ts(t, P)], start=(c == 0), stop=(c == IC - 1))
                last.then_inc(g_done, 1)

            def scores(t, b, first=False):
                pe.wait_ge(g_evac_a, 2 * t + 2)
                pe.wait_ge(g_evac_v, 2 * t + 2)
                if not first:
                    pe.wait_ge(pt_evac, 2 * t + b - 1)
                for q in range(NP):
                    last = pe.matmul(bank[2 + b][:, q * L:(q + 1) * L], GD[:, q, b, :],
                                     KVT[:, bass.ds(2 * t + b, 1), :].rearrange("p a l -> p (a l)"),
                                     start=True, stop=True)
                last.then_inc(s_done, 1)

            def transposed(t, b):
                pe.wait_ge(norm_done, 2 * t + b + 1)
                for j in range(4):
                    last = pe.transpose(bank[2 + b][:, j * P:(j + 1) * P],
                                        PR[:, b, 2 * j:2 * j + 2, :].rearrange("p q l -> p (q l)"), IDN[:, :])
                last.then_inc(pt_done, 1)

            def attend(t, b, first=False):
                pe.wait_ge(pt_evac, 2 * t + b + 1)
                pe.wait_ge(bd_ready, t + 1)
                if not first or b:
                    pe.wait_ge(ctx_evac, 2 * t + b)
                pe.matmul(bank[4][:, :], BD[:, b, :], PT[:, b, :], start=True, stop=True).then_inc(ctx_done, 1)

            def project(t, first=False):
                pe.wait_ge(ctx_evac, 2 * t + 2)
                if not first:
                    pe.wait_ge(x1_done, t)
                for q in range(NP):
                    last = pe.matmul(bank[5][:, 0:D], CT[:, q, :], N[:, q, :], start=(q == 0), stop=(q == NP - 1))
                last.then_inc(out_done, 1)

            def route(t, first=False):
                pe.wait_ge(l2_done, t + 1)
                if not first:
                    pe.wait_ge(xt2_evac, t)
                for c in range(IC):
                    last = pe.transpose(bank[6][:, c * P:(c + 1) * P], XN2[:, c * P:(c + 1) * P], IDN[:, :])
                last.then_inc(xt2_done, 1)

            def logits(t, first=False):
                pe.wait_ge(xt2_evac, t + 1)
                if not first:
                    pe.wait_ge(lg_read, t)
                for c in range(IC):
                    last = pe.matmul(bank[7][:, 0:E], XN2C[:, c, :], RW[:, c, :],
                                     start=(c == 0), stop=(c == IC - 1))
                last.then_inc(lg_done, 1)

            def tile(t, first=False, second=False, last=False):
                scores(t, 0, first)
                scores(t, 1, first)
                if not first:
                    project(t - 1, second)
                transposed(t, 0)
                if not last:
                    queries(t + 1, 0)
                attend(t, 0, first)
                transposed(t, 1)
                if not first:
                    route(t - 1, second)
                if not last:
                    queries(t + 1, 1)
                if not first:
                    logits(t - 1, second)
                attend(t, 1, first)

            pe.wait_ge(m_evac, 4)
            pe.wait_ge(n_evac, 4)
            pe.wait_ge(ld["router"], 48)
            queries(0, 0, True)
            queries(0, 1, True)
            tile(0, first=True)
            tile(1, second=True)
            with pe.Fori(2, T - 1) as t:
                tile(t)
            tile(T - 1, last=True)
            project(T - 1)
            route(T - 1)
            logits(T - 1)

            pe.wait_ge(ld["wgu"], 16)
            pe.wait_ge(ld["wd"], 16)
            pe.wait_ge(xt2_kept, T)

            def expert(e, first=False):
                for t in range(T + 2):
                    if t < T:
                        if not first or t >= 2:
                            pe.wait_ge(act_done, T * e + t - 1)
                        for c in range(IC):
                            w = WGU[:, 0, c, :] if first else WGU[:, bass.ds(e, 1), c, :].rearrange("p a f -> p (a f)")
                            last = pe.matmul(bank[t % 2][:, 0:2 * F], XN2T[:, c, t * P:(t + 1) * P], w,
                                             start=(c == 0), stop=(c == IC - 1))
                        last.then_inc(gu_done, 1)
                    if 1 <= t <= T:
                        u = t - 1
                        pe.wait_ge(act_done, T * e + u + 1)
                        if not first or u >= 2:
                            pe.wait_ge(at_evac, T * e + u - 1)
                        for c in range(2):
                            last = pe.transpose(bank[2 + u % 2][0:FH, c * P:(c + 1) * P],
                                                AC[:, u % 2, c * FH:(c + 1) * FH], IDN[:, :])
                        last.then_inc(at_done, 1)
                    if t > 1:
                        u = t - 2
                        pe.wait_ge(at_evac, T * e + u + 1)
                        if not first or u >= 2:
                            pe.wait_ge(y_added, T * e + u - 1)
                        for c in range(2):
                            w = WD[:, 0, c, :] if first else WD[:, bass.ds(e, 1), c, :].rearrange("p a f -> p (a f)")
                            last = pe.matmul(bank[4 + u % 2][:, 0:D], ACT_T[:, u % 2, c, :], w,
                                             start=(c == 0), stop=(c == 1))
                        last.then_inc(y_done, 1)

            expert(0, True)
            with pe.Fori(1, E) as e:
                expert(e)


_OUT = ((B, S, D), "float32")


def kernel(**inputs):
    import concourse.bacc as bacc
    from concourse.bass_utils import run_bass_kernel_spmd

    a = {k: np.asarray(v) for k, v in inputs.items()}

    def w(name):
        return a["L0_xattn_" + name]

    def f(name):
        return a["L0_ffn_" + name]

    inv = (np.float32(1.0) / np.float32(10000.0) ** (np.arange(0, DC, 2, dtype=np.float32) / np.float32(DC))).astype(np.float32)
    ang = np.arange(L, dtype=np.float32)[:, None] * inv[None, :]
    cos = np.repeat(np.cos(ang), 2, axis=-1).astype(np.float32)
    sin = np.repeat(np.sin(ang), 2, axis=-1).astype(np.float32)
    sin[:, :DC // 2] *= -1.0
    kvd = a["ctx_512"].transpose(1, 0, 2)
    arrays = {
        "x": a["x"].reshape(T, P, D).transpose(1, 0, 2),
        "ctxd": np.concatenate([kvd, kvd], axis=0),
        "rope_c": np.concatenate([cos, cos], axis=0),
        "rope_s": np.concatenate([sin, sin], axis=0),
        "wqrT": w("W_qr").transpose(2, 0, 1),
        "wkrT": w("W_kr").transpose(2, 0, 1),
        "kcqT_a": w("w_kc_q").transpose(2, 0, 1)[:P],
        "kcqT_b": w("w_kc_q").transpose(2, 0, 1)[P:],
        "wq": w("Wq").reshape(H, K, D).transpose(1, 0, 2),
        "kckv": w("w_kc_kv").transpose(1, 0, 2),
        "woT": w("Wo").reshape(D, H, K).transpose(2, 1, 0),
        "rwT": f("router_w").reshape(E, IC, P).transpose(2, 1, 0),
        "bias": np.concatenate([f("expert_bias").reshape(1, E)] * P, axis=0),
        "wgu": np.concatenate([f("gate_proj"), f("up_proj")], axis=2).reshape(E, IC, P, 2 * F).transpose(2, 0, 1, 3),
        "wd": f("down_proj").reshape(E, 2, FH, D).transpose(2, 0, 1, 3),
        "ident": np.eye(P, dtype=np.float32),
        "half": np.repeat(np.eye(2, dtype=np.float32), P // 2, axis=0),
        "iota": np.concatenate([np.arange(E, dtype=np.float32).reshape(1, E)] * P, axis=0),
    }
    arrays = {k: np.ascontiguousarray(v) for k, v in arrays.items()}
    nc = bacc.Bacc("TRN2", target_bir_lowering=False, num_devices=1)
    args = [nc.dram_tensor(k, v.shape, mybir.dt.from_np(v.dtype), kind="ExternalInput").ap() for k, v in arrays.items()]
    res = nc.dram_tensor("out", (P, T, D), F32, kind="ExternalOutput").ap()
    build(nc, *args, res)
    r = run_bass_kernel_spmd(nc, [arrays], core_ids=[0])
    return r.results[0]["out"].transpose(1, 0, 2).reshape(B, S, D)
```

```python
from contextlib import ExitStack

import numpy as np

import concourse.bass as bass
from concourse import mybir

F32 = mybir.dt.float32
F16 = mybir.dt.float16
I32 = mybir.dt.int32
U32 = mybir.dt.uint32
ALU = mybir.AluOpType
ACT = mybir.ActivationFunctionType
AX = mybir.AxisListType

P = 128
B, S, D = 16, 64, 256
L, DC = 64, 64
H, K, CQ, R = 16, 128, 192, 64
E, F, TOPK = 16, 224, 4
T = B * S // P
IC = D // P
FH = F // 2
NP = H // 2
EPS = 1e-5
XR = D + E
NT = (B * S * TOPK - E) // P + E
UN = 4
NG = -(-NT // UN)
AHEAD = 3
BEHIND = 2
NOWHERE = 8192

C_IDN, C_ROPE_C, C_ROPE_S, C_HALF, C_IOTA, C_STEP, C_BELOW, C_G, C_TRI, C_END = (
    int(v) for v in np.cumsum([0, P, DC, DC, 2, P, T, E * E, 1, P]))


def build(nc, x, ctxd, const, wqrT, wkrT, kcqT_a, kcqT_b, wq, kckv, woT, rwT, bias, wgu, wd, out):
    with ExitStack() as es:
        def sb(name, shape, dt=F32):
            return es.enter_context(nc.sbuf_tensor(name, shape, dt))

        def sem(name):
            return es.enter_context(nc.semaphore(name))

        X = sb("X", [P, T, D])
        XN = sb("XN", [P, T, D])
        XNT = sb("XNT", [P, IC, T * P])
        KVD = sb("KVD", [P, B, DC])
        CN = sb("CN", [P, C_END])
        IDN = CN[:, C_IDN:C_IDN + P]
        RC = CN[:, C_ROPE_C:C_ROPE_C + DC]
        RS = CN[:, C_ROPE_S:C_ROPE_S + DC]
        HALF = CN[:, C_HALF:C_HALF + 2]
        IOTA = CN[:, C_IOTA:C_IOTA + E]
        IOTAP = CN[:, C_IOTA:C_IOTA + P]
        STEP = CN[:, C_STEP:C_STEP + T]
        BELOW = CN[:, C_BELOW:C_BELOW + E * E].rearrange("p (e f) -> p e f", e=E)
        GCOL = CN[:, C_G:C_G + 1]
        KR = sb("KR", [P, B, DC])
        KVT = sb("KVT", [P, B, L])
        BD = sb("BD", [P, 2, P])
        QREG = sb("QREG", [P, H * CQ])
        WQR = QREG[0:R, :].rearrange("p (h q) -> p h q", h=H)
        WKR = sb("WKR", [R, H, DC])
        WORK = sb("WORK", [P, 2 * H * K])
        KCA = WORK[:, 0:H * K].rearrange("p (h k) -> p h k", h=H)
        KCB = WORK[0:CQ - P, H * K:].rearrange("p (h k) -> p h k", h=H)
        STAGE = sb("STAGE", [P, 2 * H * D])
        WQ = STAGE[:, 0:H * D].rearrange("p (h i) -> p h i", h=H)
        WO = STAGE[:, H * D:].rearrange("p (h i) -> p h i", h=H)
        WD = STAGE[0:FH, :].rearrange("p (e c i) -> p e c i", e=E, c=2)
        KCKV = sb("KCKV", [P, H, DC])
        CA = sb("CA", [P, H, DC])
        CB = sb("CB", [CQ - P, H, DC])
        EK = sb("EK", [P, H, DC])
        KT1 = EK
        M = sb("M", [P, IC, H, DC])
        N = sb("N", [P, NP, D])
        GD = QREG[:, 0:NP * 2 * P].rearrange("p (q b n) -> p q b n", q=NP, b=2)
        PR = WORK[:, 0:1024].rearrange("p (b q l) -> p b q l", b=2, q=NP)
        PT = WORK[:, 1024:2048].rearrange("p (b n) -> p b n", b=2)
        CT = WORK[:, 2048:3072].rearrange("p (q n) -> p q n", q=NP)
        MX = sb("MX", [P, 2, NP])
        SM = sb("SM", [P, 2, NP])
        RI = sb("RI", [P, 2, NP])
        ST6 = sb("ST6", [P, T, 6])
        MV = sb("MV", [P, T, 2])
        VE = sb("VE", [P, T])
        RSTD = sb("RSTD", [P, T])
        ST62 = sb("ST62", [P, 6])
        MV2 = sb("MV2", [P, 2])
        VE2 = sb("VE2", [P, 1])
        RSTD2 = sb("RSTD2", [P, 1])
        MH = sb("MH", [P, 1])
        XE = sb("XE", [P, XR])
        XN2 = XE[:, 0:D]
        XN2C = sb("XN2C", [P, IC, P])
        RW = sb("RW", [P, IC, E])
        BI = sb("BI", [P, E])
        LG = sb("LG", [P, E])
        M8 = sb("M8", [P, 8])
        I8 = sb("I8", [P, 8], U32)
        I4F = sb("I4F", [P, TOPK])
        D4 = sb("D4", [P, TOPK])
        W4 = sb("W4", [P, TOPK])
        S4 = sb("S4", [P, 1])
        R4 = sb("R4", [P, 1])
        OH = sb("OH", [P, TOPK, E])
        OW = sb("OW", [P, TOPK, E])
        MT = sb("MT", [P, E], F16)
        IOTAH = sb("IOTAH", [P, P], F16)
        TRI = sb("TRI", [P, P], F16)
        ONES = sb("ONES", [P, P], F16)
        RUN = sb("RUN", [P, E])
        RK = sb("RK", [P, E])
        RK4 = sb("RK4", [P, TOPK])
        RI4 = sb("RI4", [P, TOPK], I32)
        J4 = sb("J4", [P, TOPK], I32)
        S4I = sb("S4I", [P, TOPK], I32)
        S4F = sb("S4F", [P, TOPK])
        EJ4 = sb("EJ4", [P, TOPK])
        TOK = sb("TOK", [P, 1])
        OHS = sb("OHS", [P, TOPK, P], F16)
        VEJ = sb("VEJ", [P, TOPK, P], F16)
        CMP = sb("CMP", [P, E, T])
        TE = sb("TE", [P, E])
        CUM = sb("CUM", [P, E, E])
        CI = sb("CI", [P, E])
        FL = sb("FL", [P, 2, E])
        EG = sb("EG", [P, 4])
        TAB = sb("TAB", [1, P], I32)
        INVT = sb("INVT", [P, P])
        OHC = sb("OHC", [P, P])
        OHCT = sb("OHCT", [P, P])
        INVF = sb("INVF", [P, NT])
        INVZ = sb("INVZ", [P, NT])
        SLOT = sb("SLOT", [P, NG * UN + AHEAD + BEHIND, 2], U32)
        IDX = sb("IDX", [P, UN, 2], U32)
        XG = XN[:, 0:5, :].rearrange("p t i -> p (t i)")[:, 0:UN * XR].rearrange("p (u i) -> p u i", u=UN)
        XGT = XN[:, 5:7, :].rearrange("p t (c n) -> p t c n", c=IC)
        YW = WORK[:, 0:UN * D].rearrange("p (u i) -> p u i", u=UN)
        WC = sb("WC", [P, UN])
        ZERO = sb("ZERO", [P, D])
        WGU = sb("WGU", [P, E, IC, 2 * F])
        SG = WORK[:, 3072:3072 + 2 * F].rearrange("p (b f) -> p b f", b=2)
        AC = WORK[:, 3584:3584 + 2 * F].rearrange("p (b f) -> p b f", b=2)
        ACT_T = CA[0:FH, :, :].rearrange("p h d -> p (h d)")[:, 0:4 * P].rearrange("p (b c n) -> p b c n", b=2, c=2)
        bank = [es.enter_context(nc.psum_tensor(f"bank{i}", [P, 512], F32)) for i in range(8)]

        ld = {n: sem(f"ld_{n}") for n in ("x", "kv", "const", "qr", "kc0", "kc1", "wq0", "wq1", "kckv", "wo0", "wo1",
                                          "router", "wgu", "wd")}
        absorb_done = sem("absorb_done")
        setup = sem("setup")
        ln_stats, ln_aggr, ln_eps, ln_rstd, ln_done = (sem(n) for n in ("ln_stats", "ln_aggr", "ln_eps", "ln_rstd", "ln_done"))
        ropa, ropb, ropc = sem("rope_cos"), sem("rope_sin"), sem("rope_done")
        xt_done, xt_evac = sem("xt_done"), sem("xt_evac")
        kvt_done, kvt_evac = sem("kvt_done"), sem("kvt_evac")
        c_done, c_evac = sem("c_done"), sem("c_evac")
        ek_done, ek_evac = sem("ek_done"), sem("ek_evac")
        m_done, m_evac = sem("m_done"), sem("m_evac")
        n_done, n_evac = sem("n_done"), sem("n_evac")
        g_done, g_evac_a, g_evac_v = sem("g_done"), sem("g_evac_act"), sem("g_evac_dve")
        s_done, max_done, sub_done, exp_done = sem("s_done"), sem("max_done"), sem("sub_done"), sem("exp_done")
        sum_done, rcp_done, norm_done = sem("sum_done"), sem("rcp_done"), sem("norm_done")
        pt_done, pt_evac = sem("pt_done"), sem("pt_evac")
        bd_ready = sem("bd_ready")
        ctx_done, ctx_evac = sem("ctx_done"), sem("ctx_evac")
        out_done, x1_done = sem("out_done"), sem("x1_done")
        l2_stats, l2_aggr, l2_eps, l2_rstd, l2_done = (sem(n) for n in ("l2_stats", "l2_aggr", "l2_eps", "l2_rstd", "l2_done"))
        xt2_done, xt2_evac = sem("xt2_done"), sem("xt2_evac")
        ej_done, tok_done, rk_read = sem("ej_done"), sem("tok_done"), sem("rk_read")
        lg_done, lg_read, rt = sem("lg_done"), sem("lg_read"), sem("router_step")
        top_exp, xtra, wt_done = sem("top_exp"), sem("weights_step"), sem("weights_done")
        casts, mt_done, rk_done, rk = sem("casts"), sem("mt_done"), sem("rk_done"), sem("rank_step")
        ohs_done, inv_done, tb, tab_done, tab_ready = sem("ohs_done"), sem("inv_done"), sem("table_step"), sem("tab_done"), sem("tab_ready")
        slots_ready, row_stored, x1_stored, zeroed = sem("slots_ready"), sem("row_stored"), sem("x1_stored"), sem("zeroed")
        idx_ready, gathered = sem("idx_ready"), [sem(f"gathered{k}") for k in range(UN)]
        xg_done, xg_evac = sem("xg_done"), sem("xg_evac")
        scaled, added, merged = sem("scaled"), [sem("added_even"), sem("added_odd")], sem("merged")
        gu_done, silu_done, act_done = sem("gu_done"), sem("silu_done"), sem("act_done")
        at_done, at_evac = sem("at_done"), sem("at_evac")
        y_done, wc_done, spread = sem("y_done"), sem("wc_done"), sem("spread_step")

        rows = nc.dram_tensor("rows", (B * S, XR), F32, kind="Internal").ap()
        odd = nc.dram_tensor("odd", (B * S, D), F32, kind="Internal").ap()

        def nth_gather(q, j):
            return 16 * (q + j // UN + 1)

        def nth_add(q, j):
            return 16 * (UN // 2 * q + j // 2 + 1)

        def outside(g):
            return isinstance(g, int) and not 0 <= g < NT

        def experts(engine, g, n):
            _, e = nc.values_load_multi_w_load_instructions(
                TAB[0:1, bass.ds(g, n)], engines=(engine,), min_val=0, max_val=E - 1,
                skip_runtime_bounds_check_because="the table's entries are minima with E - 1")
            return list(e)

        def positive(n):
            return not isinstance(n, int) or n > 0

        block = es.enter_context(nc.Block())

        @block.sync
        def _(sp):
            sp.dma_start(X[:, :, :], x).then_inc(ld["x"], 16)
            sp.dma_start(KVD[:, :, :], ctxd).then_inc(ld["kv"], 16)
            sp.dma_start(CN[:, :], const).then_inc(ld["const"], 16)
            sp.dma_start(WQR[:, :, :], wqrT).then_inc(ld["qr"], 16)
            sp.dma_start(WKR[:, :, :], wkrT).then_inc(ld["qr"], 16)
            for g in range(2):
                h = slice(8 * g, 8 * g + 8)
                sp.dma_start(KCA[:, h, :], kcqT_a[:, h, :]).then_inc(ld[f"kc{g}"], 16)
                sp.dma_start(KCB[:, h, :], kcqT_b[:, h, :]).then_inc(ld[f"kc{g}"], 16)
            for g in range(2):
                sp.dma_start(WQ[:, 8 * g:8 * g + 8, :], wq[:, 8 * g:8 * g + 8, :]).then_inc(ld[f"wq{g}"], 16)
            sp.dma_start(KCKV[:, :, :], kckv).then_inc(ld["kckv"], 16)
            for g in range(2):
                sp.dma_start(WO[:, 8 * g:8 * g + 8, :], woT[:, 8 * g:8 * g + 8, :]).then_inc(ld[f"wo{g}"], 16)
            for dst, src in ((RW, rwT),):
                sp.dma_start(dst[:, :, :], src).then_inc(ld["router"], 16)
            sp.dma_start(BI[:, :], bias).then_inc(ld["router"], 16)
            sp.dma_start(WGU[:, :, :, :], wgu).then_inc(ld["wgu"], 16)
            sp.wait_ge(m_done, 4)
            sp.wait_ge(n_done, 4)
            sp.dma_start(WD, wd).then_inc(ld["wd"], 16)
            sp.wait_ge(setup, 3)
            sp.dma_start(odd.rearrange("(t p) i -> p t i", p=P), ZERO[:, :].unsqueeze(1).to_broadcast([P, T, D])).then_inc(zeroed, 16)
            with sp.Fori(0, T) as t:
                sp.wait_ge(x1_done, t + 1)
                sp.dma_start(out[bass.ts(t, P), :], X[:, bass.ds(t, 1), :].rearrange("p a i -> p (a i)")).then_inc(x1_stored, 16)
                sp.wait_ge(wt_done, t + 1)
                sp.wait_ge(l2_done, t + 1)
                sp.dma_start(rows[bass.ts(t, P), :], XE[:, :]).then_inc(row_stored, 16)

        @block.gpsimd
        def _(gp):
            gp.memset(MH[:, :], -0.5).then_inc(setup, 1)
            gp.memset(ZERO[:, :], 0.0).then_inc(setup, 1)
            gp.wait_ge(ld["kv"], 16)
            gp.wait_ge(ld["const"], 16)
            hd = DC // 2
            for lo in (0, hd):
                src = hd - lo
                gp.tensor_tensor(KT1[:, :, lo:lo + hd], KVD[:, :, src:src + hd],
                                 RS[:, lo:lo + hd].unsqueeze(1).to_broadcast([P, B, hd]), ALU.mult).then_inc(ropa, 1)
            gp.tensor_tensor(KR[:, :, :], KVD[:, :, :], RC[:, :].unsqueeze(1).to_broadcast([P, B, DC]),
                             ALU.mult).then_inc(ropa, 1)
            gp.wait_ge(ropa, 3)
            gp.tensor_tensor(KR[:, :, :], KR[:, :, :], KT1[:, :, :], ALU.add).then_inc(ropc, 1)
            gp.wait_ge(setup, 2)
            gp.wait_ge(ln_eps, 1)
            gp.tensor_tensor(RSTD[:, :], VE[:, :], MH[:, :].to_broadcast([P, T]), ALU.pow).then_inc(ln_rstd, 1)
            gp.wait_ge(ropc, 1)
            gp.wait_ge(c_done, 2)
            gp.memset(GD[:, :, :, :], 0.0).then_inc(setup, 1)

            def tile(t, first=False):
                if not first:
                    gp.wait_ge(ctx_done, 2 * t)
                gp.tensor_tensor(BD[:, :, :].rearrange("p b (c d) -> p b c d", c=2),
                                 KR[:, bass.ds(2 * t, 2), :].unsqueeze(2).to_broadcast([P, 2, 2, DC]),
                                 HALF[:, :].unsqueeze(1).unsqueeze(3).to_broadcast([P, 2, 2, DC]),
                                 ALU.mult).then_inc(bd_ready, 1)

            def rstd2(t):
                gp.wait_ge(l2_eps, t + 1)
                gp.tensor_tensor(RSTD2[:, :], VE2[:, :], MH[:, :], ALU.pow).then_inc(l2_rstd, 1)

            tile(0, first=True)
            with gp.Fori(1, T) as t:
                tile(t)
                rstd2(t - 1)
            rstd2(T - 1)

            gp.wait_ge(row_stored, 16 * T)
            gp.wait_ge(x1_stored, 16 * T)
            gp.wait_ge(zeroed, 16)

            gp.wait_ge(slots_ready, 1)

            def met(*waits):
                waits = [(s, n if isinstance(n, int) else gp.to_reg(n)) for s, n in waits if positive(n)]
                gp.wait_ge(zeroed, 16)
                for s, n in waits:
                    gp.wait_ge(s, n)

            def gather(q, j, rows_of):
                k = j % UN
                g = UN * q + j
                if outside(g):
                    return
                met((xg_done, g - UN + 1), (wc_done, g - UN + 1), (idx_ready, g - AHEAD + 1))
                gp.indirect_dma_start(out=XG[:, k, :], out_offset=None, in_=rows,
                                      in_offset=bass.IndirectOffsetOnAxis(ap=rows_of, axis=0)).then_inc(gathered[k], 16)

            def add(q, j, rows_of):
                g = UN * q + j
                if outside(g):
                    return
                met((scaled, g + 1), (added[j % 2], nth_add(q, j - 2)))
                gp.indirect_dma_start(out=out if j % 2 == 0 else odd,
                                      out_offset=bass.IndirectOffsetOnAxis(ap=rows_of, axis=0),
                                      in_=YW[:, j % UN, :], in_offset=None, bounds_check=B * S - 1, oob_is_err=False,
                                      compute_op=ALU.add).then_inc(added[j % 2], 16)

            for j in range(AHEAD):
                gather(0, j, SLOT[:, j, 0:1])

            def body(q):
                for k in range(UN):
                    gather(q, k + AHEAD, IDX[:, k, 0:1])
                    add(q, k - BEHIND, IDX[:, k, 1:2])

            body(0)
            with gp.Fori(1, NG - 1) as q:
                body(q)
            body(NG - 1)
            for j in range(NG * UN - BEHIND, NT):
                add(0, j, IDX[:, j % UN, 1:2])
            for k in range(2):
                gp.wait_ge(added[k], 16 * ((NT + 1 - k) // 2))
            gp.dma_start(out.rearrange("(t p) i -> p t i", p=P), odd.rearrange("(t p) i -> p t i", p=P),
                         accum_op=ALU.add).then_inc(merged, 16)
            gp.wait_ge(merged, 16)

        @block.scalar
        def _(act):
            def evac(dst, src):
                return act.activation(dst, src, ACT.Copy)
            for q in range(4):
                act.wait_ge(xt_done, q + 1)
                evac(XNT[:, :, 2 * q * P:(2 * q + 2) * P],
                     bank[q][:, :].rearrange("p (c n) -> p c n", c=IC)).then_inc(xt_evac, 1)
            for q in range(2):
                act.wait_ge(kvt_done, q + 1)
                evac(KVT[:, 8 * q:8 * q + 8, :],
                     bank[4 + q][:, :].rearrange("p (b l) -> p b l", b=8)).then_inc(kvt_evac, 1)
            for g in range(2):
                h = slice(8 * g, 8 * g + 8)
                act.wait_ge(c_done, g + 1)
                evac(CA[:, h, :], bank[g][:, :].rearrange("p (h d) -> p h d", h=8)).then_inc(c_evac, 1)
                evac(CB[:, h, :], bank[2 + g][0:CQ - P, :].rearrange("p (h d) -> p h d", h=8)).then_inc(c_evac, 1)
            for g in range(2):
                act.wait_ge(ek_done, g + 1)
                evac(EK[:, 8 * g:8 * g + 8, :],
                     bank[4 + g][:, :].rearrange("p (h d) -> p h d", h=8)).then_inc(ek_evac, 1)
            for g in range(4):
                act.wait_ge(m_done, g + 1)
                evac(M[:, :, 4 * g:4 * g + 4, :],
                     bank[6 + g % 2][:, :].rearrange("p (c h d) -> p c h d", c=IC, h=4)).then_inc(m_evac, 1)
            for j in range(4):
                act.wait_ge(n_done, j + 1)
                evac(N[:, 2 * j:2 * j + 2, :], bank[j][:, :].rearrange("p (h o) -> p h o", h=2)).then_inc(n_evac, 1)
            act.wait_ge(setup, 3)

            def g_half(t, g, first=False):
                act.wait_ge(g_done, 2 * t + g + 1)
                if not first:
                    act.wait_ge(s_done, 2 * t)
                evac(GD[0:64, 4 * g:4 * g + 4, :, 0:64],
                     bank[g][0:64, :].rearrange("p (q b s) -> p q b s", q=4, b=2)).then_inc(g_evac_a, 1)

            def exp(t, b):
                act.wait_ge(sub_done, 2 * t + b + 1)
                act.activation(PR[:, b, :, :], PR[:, b, :, :], ACT.Exp).then_inc(exp_done, 1)

            def pt(t, b, first=False):
                act.wait_ge(pt_done, 2 * t + b + 1)
                if not first:
                    act.wait_ge(ctx_done, 2 * t + b - 1)
                evac(PT[:, b, :], bank[2 + b][:, :]).then_inc(pt_evac, 1)

            def xt2(t, first=False):
                act.wait_ge(xt2_done, t + 1)
                if not first:
                    act.wait_ge(lg_done, t)
                evac(XN2C[:, :, :], bank[6][:, 0:IC * P].rearrange("p (c n) -> p c n", c=IC)).then_inc(xt2_evac, 1)

            def top(t):
                act.wait_ge(rt, 6 * t + 2)
                act.activation(D4[:, :], D4[:, :], ACT.Exp, accum_out=S4[:, :]).then_inc(top_exp, 1)

            def tile(t, first=False, second=False, last=False):
                exp(t, 0)
                exp(t, 1)
                pt(t, 0, first)
                if not last:
                    g_half(t + 1, 0)
                pt(t, 1, first)
                if not last:
                    g_half(t + 1, 1)
                if not first:
                    xt2(t - 1, second)
                    top(t - 1)

            g_half(0, 0, True)
            g_half(0, 1, True)
            tile(0, first=True)
            tile(1, second=True)
            with act.Fori(2, T - 1) as t:
                tile(t)
            tile(T - 1, last=True)
            xt2(T - 1)
            top(T - 1)

            act.wait_ge(slots_ready, 1)

            def index(q, k):
                g = UN * q + k
                if isinstance(g, int) and g >= NG * UN:
                    return
                n = nth_add(q, k - UN - BEHIND)
                if positive(n):
                    act.wait_ge(added[k % 2], n)
                act.activation(IDX[:, k % UN, :], SLOT[:, bass.ds(g + AHEAD, 1), :].rearrange("p a i -> p (a i)"),
                               ACT.Copy).then_inc(idx_ready, 1)

            def rows_t(q, j):
                g = UN * q + j
                if outside(g):
                    return
                act.wait_ge(xg_done, g + 1)
                if positive(g - 1):
                    act.wait_ge(gu_done, g - 1)
                evac(XGT[:, j % 2, :, :], bank[j % 2][:, 0:IC * P].rearrange("p (c n) -> p c n", c=IC)).then_inc(xg_evac, 1)

            def silu(q, j):
                g = UN * q + j
                if outside(g):
                    return
                act.wait_ge(gu_done, g + 1)
                if positive(g - 1):
                    act.wait_ge(act_done, g - 1)
                act.activation(SG[:, j % 2, :], bank[2 + j % 2][:, 0:F], ACT.Silu).then_inc(silu_done, 1)

            def act_t(q, j):
                g = UN * q + j
                if outside(g):
                    return
                act.wait_ge(at_done, g + 1)
                if positive(g - 1):
                    act.wait_ge(y_done, g - 1)
                evac(ACT_T[:, j % 2, :, :], bank[4 + j % 2][0:FH, 0:2 * P].rearrange("p (c n) -> p c n", c=2)).then_inc(at_evac, 1)

            def body(q):
                for k in range(UN):
                    rows_t(q, k + 1)
                    index(q, k + 1)
                    silu(q, k)
                    act_t(q, k - 1)

            index(0, 0)
            rows_t(0, 0)
            body(0)
            with act.Fori(1, NG - 1) as q:
                body(q)
            body(NG - 1)

        @block.vector
        def _(dve):
            dve.wait_ge(ld["x"], 16)
            for t in range(T):
                dve.bn_stats(ST6[:, t, :], X[:, t, :]).then_inc(ln_stats, 1)
            for t in range(T):
                dve.wait_ge(ln_stats, t + 1)
                dve.bn_aggr(MV[:, t, :], ST6[:, t, :]).then_inc(ln_aggr, 1)
            dve.wait_ge(ln_aggr, T)
            dve.tensor_scalar(VE[:, :], MV[:, :, 1], EPS, None, ALU.add).then_inc(ln_eps, 1)
            dve.wait_ge(ln_rstd, 1)
            for t in range(T):
                dve.tensor_scalar(XN[:, t, :], X[:, t, :], MV[:, t, 0:1], RSTD[:, t:t + 1],
                                  ALU.subtract, ALU.mult).then_inc(ln_done, 1)
            dve.wait_ge(setup, 3)

            def g_half(t, g, first=False):
                dve.wait_ge(g_done, 2 * t + g + 1)
                if not first:
                    dve.wait_ge(s_done, 2 * t)
                dve.tensor_copy(GD[64:128, 4 * g:4 * g + 4, :, 64:128],
                                bank[g][64:128, :].rearrange("p (q b s) -> p q b s", q=4, b=2)).then_inc(g_evac_v, 1)

            def scores(t, b, first=False):
                u = 2 * t + b
                sc = bank[2 + b][:, :].rearrange("p (q l) -> p q l", q=NP)
                dve.wait_ge(s_done, u + 1)
                dve.tensor_reduce(MX[:, b, :], sc, AX.X, ALU.max).then_inc(max_done, 1)
                dve.wait_ge(max_done, u + 1)
                if not first:
                    dve.wait_ge(pt_done, u - 1)
                dve.tensor_tensor(PR[:, b, :, :], sc, MX[:, b, :].unsqueeze(2).to_broadcast([P, NP, L]),
                                  ALU.subtract).then_inc(sub_done, 1)

            def norm(t, b):
                u = 2 * t + b
                dve.wait_ge(exp_done, u + 1)
                dve.tensor_reduce(SM[:, b, :], PR[:, b, :, :], AX.X, ALU.add).then_inc(sum_done, 1)
                dve.wait_ge(sum_done, u + 1)
                dve.reciprocal(RI[:, b, :], SM[:, b, :]).then_inc(rcp_done, 1)
                dve.wait_ge(rcp_done, u + 1)
                dve.tensor_tensor(PR[:, b, :, :], PR[:, b, :, :], RI[:, b, :].unsqueeze(2).to_broadcast([P, NP, L]),
                                  ALU.mult).then_inc(norm_done, 1)

            def latent(t, b, first=False):
                dve.wait_ge(ctx_done, 2 * t + b + 1)
                if not first:
                    dve.wait_ge(out_done, t)
                dve.tensor_copy(CT[:, :, 64 * b:64 * b + 64],
                                bank[4][:, :].rearrange("p (q s) -> p q s", q=NP)).then_inc(ctx_evac, 1)

            def wait_alone(s, n):
                dve.wait_ge(setup, 3)
                dve.wait_ge(s, n)

            def residual(t):
                dve.wait_ge(out_done, t + 1)
                xt = X[:, bass.ds(t, 1), :].rearrange("p a i -> p (a i)")
                dve.tensor_tensor(xt, bank[5][:, 0:D], xt, ALU.add).then_inc(x1_done, 1)
                wait_alone(x1_done, t + 1)
                dve.bn_stats(ST62[:, :], xt).then_inc(l2_stats, 1)
                wait_alone(l2_stats, t + 1)
                dve.bn_aggr(MV2[:, :], ST62[:, :]).then_inc(l2_aggr, 1)
                dve.wait_ge(l2_aggr, t + 1)
                dve.tensor_scalar(VE2[:, :], MV2[:, 1:2], EPS, None, ALU.add).then_inc(l2_eps, 1)

            def norm2(t, first=False):
                dve.wait_ge(l2_rstd, t + 1)
                if not first:
                    dve.wait_ge(xt2_done, t)
                    dve.wait_ge(row_stored, 16 * t)
                xt = X[:, bass.ds(t, 1), :].rearrange("p a i -> p (a i)")
                dve.tensor_scalar(XN2[:, :], xt, MV2[:, 0:1], RSTD2[:, :], ALU.subtract, ALU.mult).then_inc(l2_done, 1)

            def router(t):
                r = 6 * t
                dve.wait_ge(lg_done, t + 1)
                dve.tensor_tensor(LG[:, :], bank[5][:, 0:E], BI[:, :], ALU.add).then_inc(lg_read, 1)
                wait_alone(lg_read, t + 1)
                dve.max(M8[:, :], LG[:, :]).then_inc(rt, 1)
                dve.wait_ge(rt, r + 1)
                dve.tensor_scalar(D4[:, :], M8[:, 0:TOPK], M8[:, 0:1], None, ALU.subtract).then_inc(rt, 1)
                dve.max_index(I8[:, :], M8[:, :], LG[:, :]).then_inc(rt, 1)
                dve.wait_ge(rt, r + 3)
                dve.tensor_copy(I4F[:, :], I8[:, 0:TOPK]).then_inc(rt, 1)
                dve.wait_ge(rt, r + 4)
                dve.tensor_tensor(OH[:, :, :], IOTA.unsqueeze(1).to_broadcast([P, TOPK, E]),
                                  I4F[:, :].unsqueeze(2).to_broadcast([P, TOPK, E]), ALU.is_equal).then_inc(rt, 1)
                dve.wait_ge(rt, r + 5)
                with nc.allow_low_precision(reason="a sum of at most one 1 is exact"):
                    dve.tensor_reduce(MT[:, :], OH[:, :, :].rearrange("p k e -> p e k"), AX.X, ALU.add).then_inc(mt_done, 1)
                dve.wait_ge(top_exp, t + 1)
                dve.reciprocal(R4[:, :], S4[:, :]).then_inc(rt, 1)
                dve.wait_ge(rt, r + 6)
                dve.tensor_scalar(W4[:, :], D4[:, :], R4[:, :], None, ALU.mult).then_inc(xtra, 1)
                dve.wait_ge(xtra, 2 * t + 1)
                dve.tensor_tensor(OW[:, :, :], OH[:, :, :], W4[:, :].unsqueeze(2).to_broadcast([P, TOPK, E]),
                                  ALU.mult).then_inc(xtra, 1)
                dve.wait_ge(xtra, 2 * t + 2)
                dve.tensor_reduce(XE[:, D:XR], OW[:, :, :].rearrange("p k e -> p e k"), AX.X, ALU.add).then_inc(wt_done, 1)
                dve.wait_ge(wt_done, t + 1)

            def rank(t, first=False):
                r = 7 * t
                dve.wait_ge(rk_done, t + 1)
                dve.tensor_tensor(RK[:, :], bank[6][:, 256:256 + E], RUN[:, :], ALU.add).then_inc(rk, 1)
                dve.wait_ge(rk, r + 1)
                dve.tensor_tensor(RUN[:, :], bank[6][:, 256 + E:256 + 2 * E], RUN[:, :], ALU.add).then_inc(rk_read, 1)
                dve.tensor_tensor(OW[:, :, :], OH[:, :, :], RK[:, :].unsqueeze(1).to_broadcast([P, TOPK, E]),
                                  ALU.mult).then_inc(rk, 1)
                dve.wait_ge(rk, r + 2)
                dve.tensor_reduce(RK4[:, :], OW[:, :, :], AX.X, ALU.add).then_inc(rk, 1)
                dve.wait_ge(rk, r + 3)
                dve.tensor_copy(RI4[:, :], RK4[:, :]).then_inc(rk, 1)
                dve.wait_ge(rk, r + 4)
                dve.tensor_scalar(J4[:, :], RI4[:, :], 7, None, ALU.arith_shift_right).then_inc(rk, 1)
                dve.tensor_scalar(S4I[:, :], RI4[:, :], P - 1, None, ALU.bitwise_and).then_inc(rk, 1)
                dve.wait_ge(rk, r + 6)
                dve.tensor_copy(S4F[:, :], S4I[:, :]).then_inc(rk, 1)
                dve.scalar_tensor_tensor(EJ4[:, :], I4F[:, :], float(T), J4[:, :], ALU.mult, ALU.add).then_inc(ej_done, 1)
                dve.wait_ge(rk, r + 7)
                if not first:
                    dve.wait_ge(inv_done, t)
                for k in range(TOPK):
                    dve.tensor_scalar(OHS[:, k, :], IOTAH[:, :], S4F[:, k:k + 1], None, ALU.is_equal).then_inc(ohs_done, 1)
                dve.wait_ge(ej_done, t + 1)
                for k in range(TOPK):
                    dve.tensor_scalar(VEJ[:, k, :], IOTAH[:, :], EJ4[:, k:k + 1], TOK[:, :],
                                      ALU.is_equal, ALU.mult).then_inc(ohs_done, 1)
                dve.wait_ge(ohs_done, 8 * t + 8)
                dve.tensor_scalar(TOK[:, :], TOK[:, :], float(P), None, ALU.add).then_inc(tok_done, 1)

            def tile(t, first=False, second=False, last=False, third=False):
                scores(t, 0, first)
                scores(t, 1, first)
                if not first:
                    residual(t - 1)
                norm(t, 0)
                norm(t, 1)
                if not first:
                    norm2(t - 1, second)
                if not last:
                    g_half(t + 1, 0)
                latent(t, 0, first)
                if not (first or second):
                    rank(t - 2, third)
                if not last:
                    g_half(t + 1, 1)
                if not first:
                    router(t - 1)
                latent(t, 1, first)

            dve.tensor_copy(IOTAH[:, :], CN[:, C_IOTA:C_IOTA + P]).then_inc(casts, 1)
            dve.tensor_copy(TRI[:, :], CN[:, C_TRI:C_TRI + P]).then_inc(casts, 1)
            dve.memset(ONES[:, :], 1.0).then_inc(casts, 1)
            dve.memset(RUN[:, :], 0.0).then_inc(casts, 1)
            dve.memset(SLOT[:, :, :], 0).then_inc(casts, 1)
            dve.tensor_scalar(TOK[:, :], GCOL, 1.0, None, ALU.add).then_inc(casts, 1)
            dve.wait_ge(casts, 6)
            dve.wait_ge(ld["router"], 32)
            g_half(0, 0, True)
            g_half(0, 1, True)
            tile(0, first=True)
            tile(1, second=True)
            tile(2, third=True)
            with dve.Fori(3, T - 1) as t:
                tile(t)
            tile(T - 1, last=True)
            residual(T - 1)
            norm2(T - 1)
            rank(T - 2)
            router(T - 1)
            rank(T - 1)

            dve.wait_ge(rk_read, T)
            steps = [0]

            def table(ins):
                steps[0] += 1
                ins.then_inc(tb, 1)
                dve.wait_ge(tb, steps[0])

            table(dve.tensor_tensor(CMP[:, :, :], RUN[:, :].unsqueeze(2).to_broadcast([P, E, T]),
                                    STEP.unsqueeze(1).to_broadcast([P, E, T]), ALU.is_gt))
            table(dve.tensor_reduce(TE[:, :], CMP[:, :, :], AX.X, ALU.add))
            table(dve.tensor_tensor(CUM[:, :, :], TE[:, :].unsqueeze(1).to_broadcast([P, E, E]), BELOW, ALU.mult))
            table(dve.tensor_reduce(CI[:, :], CUM[:, :, :], AX.X, ALU.add))
            table(dve.tensor_tensor(CI[:, :], CI[:, :], TE[:, :], ALU.add))
            table(dve.tensor_scalar(FL[:, 0, :], CI[:, :], GCOL, None, ALU.is_le))
            table(dve.tensor_tensor(FL[:, 1, :], FL[:, 0, :], TE[:, :], ALU.mult))
            table(dve.tensor_reduce(EG[:, 0:2], FL[:, :, :], AX.X, ALU.add))
            table(dve.scalar_tensor_tensor(EG[:, 2:3], EG[:, 0:1], float(T), EG[:, 1:2], ALU.mult, ALU.subtract))
            table(dve.tensor_scalar(EG[:, 3:4], EG[:, 2:3], GCOL, float(P), ALU.add, ALU.min))
            table(dve.tensor_scalar(EG[:, 2:3], EG[:, 0:1], float(E - 1), None, ALU.min))
            dve.tensor_scalar(OHC[:, :], IOTAP, EG[:, 3:4], None, ALU.is_equal).then_inc(spread, 1)
            dve.wait_ge(inv_done, T)
            dve.tensor_copy(INVT[:, :], bank[7][:, 0:P]).then_inc(spread, 1)
            dve.wait_ge(tab_done, 1)
            dve.tensor_copy(OHCT[:, :], bank[6][:, P:2 * P]).then_inc(spread, 1)
            dve.tensor_copy(TAB[:, :], bank[6][0:1, 0:P]).then_inc(tab_ready, 1)
            dve.wait_ge(tab_done, 2)
            table(dve.tensor_copy(INVF[:, :], bank[5][:, 0:NT]))
            table(dve.tensor_scalar(INVZ[:, :], INVF[:, :], 0.0, float(NOWHERE), ALU.is_equal, ALU.mult))
            dve.tensor_scalar(SLOT[:, 0:NT, 0], INVF[:, :], -1.0, 0.0, ALU.add, ALU.max).then_inc(spread, 1)
            dve.scalar_tensor_tensor(SLOT[:, AHEAD + BEHIND:AHEAD + BEHIND + NT, 1], INVF[:, :], -1.0, INVZ[:, :],
                                     ALU.add, ALU.add).then_inc(spread, 1)
            dve.wait_ge(spread, 5)
            dve.sem_inc(slots_ready, 1)

            def weight(q, j, e):
                g = UN * q + j
                if outside(g):
                    return
                dve.wait_ge(gathered[j % UN], nth_gather(q, j))
                if positive(g - UN + 1):
                    dve.wait_ge(scaled, g - UN + 1)
                dve.tensor_copy(WC[:, j % UN:j % UN + 1], XG[:, j % UN, bass.ds(D + e, 1)]).then_inc(wc_done, 1)

            def product(q, j):
                g = UN * q + j
                if outside(g):
                    return
                dve.wait_ge(silu_done, g + 1)
                if positive(g - 1):
                    dve.wait_ge(at_done, g - 1)
                dve.tensor_tensor(AC[:, j % 2, :], SG[:, j % 2, :], bank[2 + j % 2][:, F:2 * F], ALU.mult).then_inc(act_done, 1)

            def weigh(q, j):
                g = UN * q + j
                if outside(g):
                    return
                dve.wait_ge(y_done, g + 1)
                dve.wait_ge(wc_done, g + 1)
                if positive(nth_add(q, j - UN)):
                    dve.wait_ge(added[j % 2], nth_add(q, j - UN))
                dve.tensor_scalar(YW[:, j % UN, :], bank[6 + j % 2][:, 0:D], WC[:, j % UN:j % UN + 1], None,
                                  ALU.mult).then_inc(scaled, 1)

            def body(q):
                e = experts(mybir.EngineType.DVE, UN * q + 1, UN)
                for k in range(UN):
                    weight(q, k + 1, e[k])
                    product(q, k)
                    weigh(q, k - BEHIND)

            weight(0, 0, experts(mybir.EngineType.DVE, 0, 1)[0])
            body(0)
            with dve.Fori(1, NG - 1) as q:
                body(q)
            body(NG - 1)
            for j in range(NG * UN - BEHIND, NT):
                weigh(0, j)

        @block.tensor
        def _(pe):
            pe.wait_ge(ld["const"], 16)
            for t in range(T):
                pe.wait_ge(ln_done, t + 1)
                for c in range(IC):
                    last = pe.transpose(bank[t // 2][:, c * 2 * P + (t % 2) * P:c * 2 * P + (t % 2 + 1) * P],
                                        XN[:, t, c * P:(c + 1) * P], IDN)
                if t % 2:
                    last.then_inc(xt_done, 1)
            pe.wait_ge(ld["qr"], 32)
            for g in range(2):
                pe.wait_ge(xt_evac, 4)
                for h in range(8 * g, 8 * g + 8):
                    o = slice((h % 8) * DC, (h % 8 + 1) * DC)
                    pe.matmul(bank[g][:, o], WQR[:, h, 0:P], WKR[:, h, :], start=True, stop=True)
                    last = pe.matmul(bank[2 + g][0:CQ - P, o], WQR[:, h, P:CQ], WKR[:, h, :], start=True, stop=True)
                last.then_inc(c_done, 1)
            pe.wait_ge(ropc, 1)
            for b in range(B):
                last = pe.matmul(bank[4 + b // 8][0:64, (b % 8) * L:(b % 8 + 1) * L], KR[0:64, b, :], IDN[0:64, 0:64],
                                 start=True, stop=True)
                last = pe.matmul(bank[4 + b // 8][64:128, (b % 8) * L:(b % 8 + 1) * L], KR[64:128, b, :],
                                 IDN[64:128, 64:128], start=True, stop=True)
                if b % 8 == 7:
                    last.then_inc(kvt_done, 1)
            for g in range(2):
                pe.wait_ge(ld[f"kc{g}"], 32)
                pe.wait_ge(c_evac, 2 * g + 2)
                pe.wait_ge(kvt_evac, g + 1)
                for h in range(8 * g, 8 * g + 8):
                    o = bank[4 + g][:, (h % 8) * DC:(h % 8 + 1) * DC]
                    pe.matmul(o, KCA[:, h, :], CA[:, h, :], start=True, stop=False)
                    last = pe.matmul(o, KCB[:, h, :], CB[:, h, :], start=False, stop=True)
                last.then_inc(ek_done, 1)
            for g in range(4):
                pe.wait_ge(ld[f"wq{g // 2}"], 16)
                pe.wait_ge(ek_evac, g // 2 + 1)
                if g >= 2:
                    pe.wait_ge(m_evac, g - 1)
                for h in range(4 * g, 4 * g + 4):
                    for c in range(IC):
                        o = (c * 4 + h % 4) * DC
                        last = pe.matmul(bank[6 + g % 2][:, o:o + DC], WQ[:, h, c * P:(c + 1) * P], EK[:, h, :],
                                         start=True, stop=True)
                last.then_inc(m_done, 1)
            pe.wait_ge(ld["kckv"], 16)
            for j in range(4):
                pe.wait_ge(ld[f"wo{j // 2}"], 16)
                pe.wait_ge(c_evac, 4)
                for p2 in range(2):
                    for h2 in range(2):
                        h = 4 * j + 2 * p2 + h2
                        last = pe.matmul(bank[j][64 * p2:64 * p2 + 64, h2 * D:(h2 + 1) * D], KCKV[:, h, :], WO[:, h, :],
                                         start=True, stop=True)
                last.then_inc(n_done, 1)

            def queries(t, g, first=False):
                if not first:
                    pe.wait_ge(g_evac_a, 2 * t + g - 1)
                    pe.wait_ge(g_evac_v, 2 * t + g - 1)
                for q in range(4):
                    for c in range(IC):
                        h = 8 * g + 2 * q
                        last = pe.matmul(bank[g][:, q * P:(q + 1) * P],
                                         M[:, c, h:h + 2, :].rearrange("p h d -> p (h d)"),
                                         XNT[:, c, bass.ts(t, P)], start=(c == 0), stop=(c == IC - 1))
                last.then_inc(g_done, 1)

            def scores(t, b, first=False):
                pe.wait_ge(g_evac_a, 2 * t + 2)
                pe.wait_ge(g_evac_v, 2 * t + 2)
                if not first:
                    pe.wait_ge(pt_evac, 2 * t + b - 1)
                for q in range(NP):
                    last = pe.matmul(bank[2 + b][:, q * L:(q + 1) * L], GD[:, q, b, :],
                                     KVT[:, bass.ds(2 * t + b, 1), :].rearrange("p a l -> p (a l)"),
                                     start=True, stop=True)
                last.then_inc(s_done, 1)

            def transposed(t, b):
                pe.wait_ge(norm_done, 2 * t + b + 1)
                for j in range(4):
                    last = pe.transpose(bank[2 + b][:, j * P:(j + 1) * P],
                                        PR[:, b, 2 * j:2 * j + 2, :].rearrange("p q l -> p (q l)"), IDN)
                last.then_inc(pt_done, 1)

            def attend(t, b, first=False):
                pe.wait_ge(pt_evac, 2 * t + b + 1)
                pe.wait_ge(bd_ready, t + 1)
                if not first or b:
                    pe.wait_ge(ctx_evac, 2 * t + b)
                pe.matmul(bank[4][:, :], BD[:, b, :], PT[:, b, :], start=True, stop=True).then_inc(ctx_done, 1)

            def project(t, first=False):
                pe.wait_ge(ctx_evac, 2 * t + 2)
                if not first:
                    pe.wait_ge(lg_read, t)
                for q in range(NP):
                    last = pe.matmul(bank[5][:, 0:D], CT[:, q, :], N[:, q, :], start=(q == 0), stop=(q == NP - 1))
                last.then_inc(out_done, 1)

            def route(t, first=False):
                pe.wait_ge(l2_done, t + 1)
                if not first:
                    pe.wait_ge(rk_read, t)
                    pe.wait_ge(xt2_evac, t)
                for c in range(IC):
                    last = pe.transpose(bank[6][:, c * P:(c + 1) * P], XN2[:, c * P:(c + 1) * P], IDN)
                last.then_inc(xt2_done, 1)

            def logits(t, first=False):
                pe.wait_ge(xt2_evac, t + 1)
                if not first:
                    pe.wait_ge(lg_read, t)
                for c in range(IC):
                    last = pe.matmul(bank[5][:, 0:E], XN2C[:, c, :], RW[:, c, :],
                                     start=(c == 0), stop=(c == IC - 1))
                last.then_inc(lg_done, 1)

            def ranks(t):
                pe.wait_ge(mt_done, t + 1)
                pe.matmul(bank[6][:, 256:256 + E], TRI[:, :], MT[:, :], start=True, stop=True)
                pe.matmul(bank[6][:, 256 + E:256 + 2 * E], ONES[:, :], MT[:, :], start=True, stop=True).then_inc(rk_done, 1)

            def invert(t, first=False, last=False):
                pe.wait_ge(ohs_done, 8 * t + 8)
                for k in range(TOPK):
                    m = pe.matmul(bank[7][:, 0:P], VEJ[:, k, :], OHS[:, k, :], start=(first and k == 0),
                                  stop=(last and k == TOPK - 1))
                m.then_inc(inv_done, 1)

            def tile(t, first=False, second=False, last=False, third=False):
                scores(t, 0, first)
                scores(t, 1, first)
                if not first:
                    project(t - 1, second)
                transposed(t, 0)
                if not last:
                    queries(t + 1, 0)
                attend(t, 0, first)
                transposed(t, 1)
                if not first:
                    route(t - 1, second)
                if not last:
                    queries(t + 1, 1)
                if not first:
                    logits(t - 1, second)
                if not (first or second):
                    invert(t - 2, third)
                attend(t, 1, first)
                if not first:
                    ranks(t - 1)

            pe.wait_ge(m_evac, 4)
            pe.wait_ge(n_evac, 4)
            pe.wait_ge(ld["router"], 32)
            queries(0, 0, True)
            queries(0, 1, True)
            tile(0, first=True)
            tile(1, second=True)
            tile(2, third=True)
            with pe.Fori(3, T - 1) as t:
                tile(t)
            tile(T - 1, last=True)
            project(T - 1)
            route(T - 1)
            logits(T - 1)

            invert(T - 2)
            ranks(T - 1)
            invert(T - 1, last=True)
            pe.wait_ge(tb, 11)
            pe.matmul(bank[6][0:1, 0:P], EG[:, 2:3], IDN, start=True, stop=True)
            pe.wait_ge(spread, 1)
            pe.transpose(bank[6][:, P:2 * P], OHC[:, :], IDN).then_inc(tab_done, 1)
            pe.wait_ge(spread, 3)
            pe.matmul(bank[5][:, 0:NT], INVT[:, :], OHCT[:, 0:NT], start=True, stop=True).then_inc(tab_done, 1)
            pe.wait_ge(tab_ready, 1)
            pe.wait_ge(ld["wgu"], 16)
            pe.wait_ge(ld["wd"], 16)

            def turn(q, j):
                g = UN * q + j
                if outside(g):
                    return
                pe.wait_ge(gathered[j % UN], nth_gather(q, j))
                if positive(g - 1):
                    pe.wait_ge(xg_evac, g - 1)
                for c in range(IC):
                    last = pe.transpose(bank[j % 2][:, c * P:(c + 1) * P], XG[:, j % UN, c * P:(c + 1) * P], IDN)
                last.then_inc(xg_done, 1)

            def gate_up(q, j, e):
                g = UN * q + j
                if outside(g):
                    return
                pe.wait_ge(xg_evac, g + 1)
                if positive(g - 1):
                    pe.wait_ge(act_done, g - 1)
                for c in range(IC):
                    last = pe.matmul(bank[2 + j % 2][:, 0:2 * F], XGT[:, j % 2, c, :],
                                     WGU[:, bass.ds(e, 1), c, :].rearrange("p a f -> p (a f)"),
                                     start=(c == 0), stop=(c == IC - 1))
                last.then_inc(gu_done, 1)

            def turn_act(q, j):
                g = UN * q + j
                if outside(g):
                    return
                pe.wait_ge(act_done, g + 1)
                if positive(g - 1):
                    pe.wait_ge(at_evac, g - 1)
                for c in range(2):
                    last = pe.transpose(bank[4 + j % 2][0:FH, c * P:(c + 1) * P], AC[:, j % 2, c * FH:(c + 1) * FH], IDN)
                last.then_inc(at_done, 1)

            def down(q, j, e):
                g = UN * q + j
                if outside(g):
                    return
                pe.wait_ge(at_evac, g + 1)
                if positive(g - 1):
                    pe.wait_ge(scaled, g - 1)
                for c in range(2):
                    last = pe.matmul(bank[6 + j % 2][:, 0:D], ACT_T[:, j % 2, c, :],
                                     WD[:, bass.ds(e, 1), c, :].rearrange("p a f -> p (a f)"),
                                     start=(c == 0), stop=(c == 1))
                last.then_inc(y_done, 1)

            def body(q, skip=0):
                e = [None] * skip + experts(mybir.EngineType.PE, UN * q - BEHIND + skip, UN + BEHIND - skip)
                for k in range(UN):
                    turn(q, k + 1)
                    gate_up(q, k, e[k + BEHIND])
                    turn_act(q, k - 1)
                    down(q, k - BEHIND, e[k])
                return e

            turn(0, 0)
            body(0, skip=BEHIND)
            with pe.Fori(1, NG - 1) as q:
                body(q)
            e = body(NG - 1)
            for j in range(NG * UN - BEHIND, NT):
                down(0, j, e[j - (NG - 1) * UN + BEHIND])


_OUT = ((B, S, D), "float32")


def kernel(**inputs):
    import concourse.bacc as bacc
    from concourse.bass_utils import run_bass_kernel_spmd

    a = {k: np.asarray(v) for k, v in inputs.items()}

    def w(name):
        return a["L0_xattn_" + name]

    def f(name):
        return a["L0_ffn_" + name]

    inv = (np.float32(1.0) / np.float32(10000.0) ** (np.arange(0, DC, 2, dtype=np.float32) / np.float32(DC))).astype(np.float32)
    ang = np.arange(L, dtype=np.float32)[:, None] * inv[None, :]
    cos = np.repeat(np.cos(ang), 2, axis=-1).astype(np.float32)
    sin = np.repeat(np.sin(ang), 2, axis=-1).astype(np.float32)
    sin[:, :DC // 2] *= -1.0
    below = np.tril(np.ones((E, E), np.float32), -1)
    ahead = np.triu(np.ones((P, P), np.float32), 1)
    const = np.concatenate([np.eye(P, dtype=np.float32), np.concatenate([cos, cos]), np.concatenate([sin, sin]),
                            np.repeat(np.eye(2, dtype=np.float32), P // 2, axis=0),
                            np.tile(np.arange(P, dtype=np.float32), (P, 1)),
                            np.tile(np.arange(T, dtype=np.float32) * P, (P, 1)),
                            np.tile(below.reshape(1, E * E), (P, 1)),
                            np.arange(P, dtype=np.float32).reshape(P, 1), ahead], axis=1)
    kvd = a["ctx_512"].transpose(1, 0, 2)
    arrays = {
        "x": a["x"].reshape(T, P, D).transpose(1, 0, 2),
        "ctxd": np.concatenate([kvd, kvd], axis=0),
        "const": const,
        "wqrT": w("W_qr").transpose(2, 0, 1),
        "wkrT": w("W_kr").transpose(2, 0, 1),
        "kcqT_a": w("w_kc_q").transpose(2, 0, 1)[:P],
        "kcqT_b": w("w_kc_q").transpose(2, 0, 1)[P:],
        "wq": w("Wq").reshape(H, K, D).transpose(1, 0, 2),
        "kckv": w("w_kc_kv").transpose(1, 0, 2),
        "woT": w("Wo").reshape(D, H, K).transpose(2, 1, 0),
        "rwT": f("router_w").reshape(E, IC, P).transpose(2, 1, 0),
        "bias": np.concatenate([f("expert_bias").reshape(1, E)] * P, axis=0),
        "wgu": np.concatenate([f("gate_proj"), f("up_proj")], axis=2).reshape(E, IC, P, 2 * F).transpose(2, 0, 1, 3),
        "wd": f("down_proj").reshape(E, 2, FH, D).transpose(2, 0, 1, 3),
    }
    arrays = {k: np.ascontiguousarray(v) for k, v in arrays.items()}
    nc = bacc.Bacc("TRN2", target_bir_lowering=False, num_devices=1)
    args = [nc.dram_tensor(k, v.shape, mybir.dt.from_np(v.dtype), kind="ExternalInput").ap() for k, v in arrays.items()]
    res = nc.dram_tensor("out", (B * S, D), F32, kind="ExternalOutput").ap()
    build(nc, *args, res)
    r = run_bass_kernel_spmd(nc, [arrays], core_ids=[0])
    return r.results[0]["out"].reshape(B, S, D)
```

```python
from contextlib import ExitStack

import numpy as np

import concourse.bass as bass
from concourse import mybir

F32 = mybir.dt.float32
F16 = mybir.dt.float16
I32 = mybir.dt.int32
U32 = mybir.dt.uint32
ALU = mybir.AluOpType
ACT = mybir.ActivationFunctionType
AX = mybir.AxisListType

P = 128
B, S, D = 16, 64, 256
L, DC = 64, 64
H, K, CQ, R = 16, 128, 192, 64
E, F, TOPK = 16, 224, 4
T = B * S // P
IC = D // P
FH = F // 2
NP = H // 2
EPS = 1e-5
XR = D + E
NT = (B * S * TOPK - E) // P + E
UN = 4
AHEAD = 3
BEHIND = 2
NG = -(-(NT + 1) // UN)
NOWHERE = 8192

C_IDN, C_ROPE_C, C_ROPE_S, C_HALF, C_IOTA, C_STEP, C_UPTO, C_G, C_TRI, C_END = (
    int(v) for v in np.cumsum([0, P, DC, DC, 2, P, T, E * E, 1, P]))


def build(nc, x, ctxd, const, wqrT, wkrT, kcqT_a, kcqT_b, wq, kckv, woT, rwT, bias, wgu, wd, out):
    with ExitStack() as es:
        def sb(name, shape, dt=F32):
            return es.enter_context(nc.sbuf_tensor(name, shape, dt))

        def sem(name):
            return es.enter_context(nc.semaphore(name))

        X = sb("X", [P, T, D])
        XN = sb("XN", [P, T, D])
        XNT = sb("XNT", [P, IC, T * P])
        KVD = sb("KVD", [P, B, DC])
        CN = sb("CN", [P, C_END])
        IDN = CN[:, C_IDN:C_IDN + P]
        RC = CN[:, C_ROPE_C:C_ROPE_C + DC]
        RS = CN[:, C_ROPE_S:C_ROPE_S + DC]
        HALF = CN[:, C_HALF:C_HALF + 2]
        IOTA = CN[:, C_IOTA:C_IOTA + E]
        IOTAP = CN[:, C_IOTA:C_IOTA + P]
        STEP = CN[:, C_STEP:C_STEP + T]
        UPTO = CN[:, C_UPTO:C_UPTO + E * E].rearrange("p (e f) -> p e f", e=E)
        GCOL = CN[:, C_G:C_G + 1]
        KR = sb("KR", [P, B, DC])
        KVT = sb("KVT", [P, B, L])
        BD = sb("BD", [P, 2, P])
        QREG = sb("QREG", [P, H * CQ])
        WQR = QREG[0:R, :].rearrange("p (h q) -> p h q", h=H)
        WKR = sb("WKR", [R, H, DC])
        WORK = sb("WORK", [P, 2 * H * K])
        KCA = WORK[:, 0:H * K].rearrange("p (h k) -> p h k", h=H)
        KCB = WORK[0:CQ - P, H * K:].rearrange("p (h k) -> p h k", h=H)
        STAGE = sb("STAGE", [P, 2 * H * D])
        WQ = STAGE[:, 0:H * D].rearrange("p (h i) -> p h i", h=H)
        WO = STAGE[:, H * D:].rearrange("p (h i) -> p h i", h=H)
        WD = STAGE[0:FH, :].rearrange("p (e c i) -> p e c i", e=E, c=2)
        KCKV = sb("KCKV", [P, H, DC])
        CA = sb("CA", [P, H, DC])
        CB = sb("CB", [CQ - P, H, DC])
        EK = sb("EK", [P, H, DC])
        M = sb("M", [P, IC, H, DC])
        N = sb("N", [P, NP, D])
        EKT = XNT[:, 1, 0:4 * P].rearrange("p (u q k) -> p u q k", u=2, q=2)
        KT1 = XNT[:, 0, :].rearrange("p (b d) -> p b d", d=DC)
        MT2 = N[:, 4:8, :].rearrange("p (u q) i -> p u q i", u=2)
        GQ = QREG[:, 0:NP * P].rearrange("p (q n) -> p q n", q=NP)
        KVS = QREG[:, NP * P:NP * P + 2 * L].rearrange("p (b l) -> p b l", b=2)
        PR = WORK[:, 0:1024].rearrange("p (b q l) -> p b q l", b=2, q=NP)
        PT = WORK[:, 1024:2048].rearrange("p (b n) -> p b n", b=2)
        CT = WORK[:, 2048:3072].rearrange("p (q n) -> p q n", q=NP)
        NM = sb("NM", [P, 2, NP])
        SM = sb("SM", [P, 2, NP])
        RI = sb("RI", [P, 2, NP])
        ST6 = sb("ST6", [P, T, 6])
        MV = sb("MV", [P, T, 2])
        VE = sb("VE", [P, T])
        RSTD = sb("RSTD", [P, T])
        ST62 = sb("ST62", [P, 6])
        MV2 = sb("MV2", [P, 2])
        VE2 = sb("VE2", [P, 1])
        RSTD2 = sb("RSTD2", [P, 1])
        MH = sb("MH", [P, 1])
        XE = sb("XE", [P, XR])
        XN2 = XE[:, 0:D]
        XN2C = sb("XN2C", [P, IC, P])
        RW = sb("RW", [P, IC, E])
        BI = sb("BI", [P, E])
        LG = sb("LG", [P, E])
        M8 = sb("M8", [P, 8])
        I8 = sb("I8", [P, 8], U32)
        I4F = sb("I4F", [P, TOPK])
        D4 = sb("D4", [P, TOPK])
        W4 = sb("W4", [P, TOPK])
        S4 = sb("S4", [P, 1])
        R4 = sb("R4", [P, 1])
        OH = sb("OH", [P, TOPK, E])
        OW = sb("OW", [P, TOPK, E])
        OR = sb("OR", [P, TOPK, E])
        MT = sb("MT", [P, E], F16)
        IOTAH = sb("IOTAH", [P, P], F16)
        TRI = sb("TRI", [P, P], F16)
        ONES = sb("ONES", [P, P], F16)
        RUN = sb("RUN", [P, E])
        RK = sb("RK", [P, E])
        RK4 = sb("RK4", [P, TOPK])
        RI4 = sb("RI4", [P, TOPK], I32)
        J4 = sb("J4", [P, TOPK], I32)
        S4I = sb("S4I", [P, TOPK], I32)
        S4F = sb("S4F", [P, TOPK])
        EJ4 = sb("EJ4", [P, TOPK])
        TOK = sb("TOK", [P, 1])
        OHS = sb("OHS", [P, TOPK, P], F16)
        VEJ = sb("VEJ", [P, TOPK, P], F16)
        CMP = sb("CMP", [P, E, T])
        TE = sb("TE", [P, E])
        TR = sb("TR", [P, E])
        CUM = sb("CUM", [P, E, E])
        CI = sb("CI", [P, E])
        FL = sb("FL", [P, 2, E])
        EG = sb("EG", [P, 4])
        TAB = sb("TAB", [1, P], I32)
        INVT = WORK[:, 0:P]
        OHC = WORK[:, P:2 * P]
        OHCT = WORK[:, 2 * P:3 * P]
        INVZ = sb("INVZ", [P, NT])
        SLOT = sb("SLOT", [P, NG * UN + AHEAD + BEHIND, 2], U32)
        IDX = sb("IDX", [P, UN, 2], U32)
        XG = XN[:, 0:5, :].rearrange("p t i -> p (t i)")[:, 0:UN * XR].rearrange("p (u i) -> p u i", u=UN)
        XGT = XN[:, 5:7, :].rearrange("p t (c n) -> p t c n", c=IC)
        YW = WORK[:, 0:UN * D].rearrange("p (u i) -> p u i", u=UN)
        WC = sb("WC", [P, UN])
        ZERO = sb("ZERO", [P, D])
        WGU = sb("WGU", [P, E, IC, 2 * F])
        SG = WORK[:, 3072:3072 + 2 * F].rearrange("p (b f) -> p b f", b=2)
        AC = WORK[:, 3584:3584 + 2 * F].rearrange("p (b f) -> p b f", b=2)
        ACT_T = CA[0:FH, :, :].rearrange("p h d -> p (h d)")[:, 0:4 * P].rearrange("p (b c n) -> p b c n", b=2, c=2)
        bank = [es.enter_context(nc.psum_tensor(f"bank{i}", [P, 512], F32)) for i in range(8)]

        ld = {n: sem(f"ld_{n}") for n in ("x", "kv", "const", "qr", "kc0", "kc1", "wq0", "wq1", "kckv", "wo0", "wo1",
                                          "router", "wgu", "wd")}
        setup = sem("setup")
        ln_stats, ln_aggr, ln_eps, ln_rstd, ln_done = (sem(n) for n in ("ln_stats", "ln_aggr", "ln_eps", "ln_rstd", "ln_done"))
        ropa, ropc = sem("rope_products"), sem("rope_done")
        xt_done, xt_evac = sem("xt_done"), sem("xt_evac")
        kvt_done, kvt_evac = sem("kvt_done"), sem("kvt_evac")
        mt2_done, mt2_evac = sem("mt2_done"), sem("mt2_evac")
        c_done, c_evac = sem("c_done"), sem("c_evac")
        kt_done, kt_evac = sem("kt_done"), sem("kt_evac")
        ek_done, ek_evac = sem("ek_done"), sem("ek_evac")
        m_done, m_evac = sem("m_done"), sem("m_evac")
        n_done, n_evac = sem("n_done"), sem("n_evac")
        g_done, g_evac = sem("g_done"), sem("g_evac")
        s_done, max_done, exp_done = sem("s_done"), sem("max_done"), sem("exp_done")
        rcp_done, norm_done = sem("rcp_done"), sem("norm_done")
        pt_done, pt_evac = sem("pt_done"), sem("pt_evac")
        bd_ready, keys_ready = sem("bd_ready"), sem("keys_ready")
        ctx_done, ctx_evac = sem("ctx_done"), sem("ctx_evac")
        out_done, x1_done = sem("out_done"), sem("x1_done")
        l2_stats, l2_aggr, l2_eps, l2_rstd, l2_done = (sem(n) for n in ("l2_stats", "l2_aggr", "l2_eps", "l2_rstd", "l2_done"))
        xt2_done, xt2_evac = sem("xt2_done"), sem("xt2_evac")
        ej_done, tok_done, rk_read = sem("ej_done"), sem("tok_done"), sem("rk_read")
        lg_done, lg_read, rt = sem("lg_done"), sem("lg_read"), sem("router_step")
        top_exp, xtra, wt_done = sem("top_exp"), sem("weights_step"), sem("weights_done")
        casts, mt_done, rk_done, rk = sem("casts"), sem("mt_done"), sem("rk_done"), sem("rank_step")
        ohs_done, inv_done, tb, tab_done, tab_ready = sem("ohs_done"), sem("inv_done"), sem("table_step"), sem("tab_done"), sem("tab_ready")
        slots_ready, row_stored, weight_stored = sem("slots_ready"), sem("row_stored"), sem("weight_stored")
        x1_stored, zeroed = sem("x1_stored"), sem("zeroed")
        idx_ready, gathered = sem("idx_ready"), [sem(f"gathered{k}") for k in range(UN)]
        xg_done, xg_evac = sem("xg_done"), sem("xg_evac")
        scaled, added, merged = sem("scaled"), [sem("added_even"), sem("added_odd")], sem("merged")
        gu_done, silu_done, act_done = sem("gu_done"), sem("silu_done"), sem("act_done")
        at_done, at_evac = sem("at_done"), sem("at_evac")
        y_done, wc_done, spread = sem("y_done"), sem("wc_done"), sem("spread_step")

        rows = nc.dram_tensor("rows", (B * S, XR), F32, kind="Internal").ap()
        odd = nc.dram_tensor("odd", (B * S, D), F32, kind="Internal").ap()

        def nth_gather(q, j):
            return 16 * (q + j // UN + 1)

        def nth_add(q, j):
            return 16 * (UN // 2 * q + j // 2 + 1)

        def no_tile(t):
            return isinstance(t, int) and not 0 <= t < T

        def outside(g):
            return isinstance(g, int) and g < 0

        def experts(engine, g, n, least=0, most=E - 1):
            _, e = nc.values_load_multi_w_load_instructions(
                TAB[0:1, bass.ds(g, n)], engines=(engine,), min_val=least, max_val=most,
                skip_runtime_bounds_check_because="the table is made of minima with E - 1 and of a count of tiles")
            return list(e)

        def tiles_used(engine):
            return experts(engine, P - 1, 1, B * S * TOPK // P, NT)[0]

        def positive(n):
            return not isinstance(n, int) or n > 0

        block = es.enter_context(nc.Block())

        @block.sync
        def _(sp):
            def heads(name, g, *transfers):
                h = slice(8 * g, 8 * g + 8)
                for dst, src in transfers:
                    sp.dma_start(dst[:, h, :], src[:, h, :]).then_inc(ld[f"{name}{g}"], 16)

            sp.dma_start(KCKV[:, :, :], kckv).then_inc(ld["kckv"], 16)
            heads("wo", 0, (WO, woT))
            sp.dma_start(WQR[:, :, :], wqrT).then_inc(ld["qr"], 16)
            sp.dma_start(WKR[:, :, :], wkrT).then_inc(ld["qr"], 16)
            heads("kc", 0, (KCA, kcqT_a), (KCB, kcqT_b))
            heads("wq", 0, (WQ, wq))
            sp.dma_start(CN[:, :], const).then_inc(ld["const"], 16)
            sp.dma_start(X[:, :, :], x).then_inc(ld["x"], 16)
            heads("kc", 1, (KCA, kcqT_a), (KCB, kcqT_b))
            sp.dma_start(KVD[:, :, :], ctxd).then_inc(ld["kv"], 16)
            heads("wq", 1, (WQ, wq))
            heads("wo", 1, (WO, woT))
            sp.dma_start(RW[:, :, :], rwT).then_inc(ld["router"], 16)
            sp.dma_start(BI[:, :], bias).then_inc(ld["router"], 16)
            sp.dma_start(WGU[:, :, :, :], wgu).then_inc(ld["wgu"], 16)
            sp.wait_ge(m_done, 4)
            sp.wait_ge(n_done, 4)
            sp.dma_start(WD, wd).then_inc(ld["wd"], 16)
            sp.wait_ge(setup, 2)
            sp.dma_start(odd.rearrange("(t p) i -> p t i", p=P), ZERO[:, :].unsqueeze(1).to_broadcast([P, T, D])).then_inc(zeroed, 16)

            def store(t):
                if not no_tile(t):
                    sp.wait_ge(x1_done, t + 1)
                    sp.dma_start(out[bass.ts(t, P), :], X[:, bass.ds(t, 1), :].rearrange("p a i -> p (a i)")).then_inc(x1_stored, 16)
                    sp.wait_ge(l2_done, t + 1)
                    sp.dma_start(rows[bass.ts(t, P), 0:D], XE[:, 0:D]).then_inc(row_stored, 16)
                if not no_tile(t - 1):
                    sp.wait_ge(wt_done, t)
                    sp.dma_start(rows[bass.ts(t - 1, P), D:XR], XE[:, D:XR]).then_inc(weight_stored, 16)

            store(0)
            with sp.Fori(1, T) as t:
                store(t)
            store(T)

        @block.gpsimd
        def _(gp):
            gp.memset(MH[:, :], -0.5).then_inc(setup, 1)
            gp.memset(ZERO[:, :], 0.0).then_inc(setup, 1)
            gp.wait_ge(setup, 2)
            gp.wait_ge(ln_eps, 1)
            gp.tensor_tensor(RSTD[:, :], VE[:, :], MH[:, :].to_broadcast([P, T]), ALU.pow).then_inc(ln_rstd, 1)
            gp.wait_ge(ropc, 1)

            def rows_twice(t):
                if no_tile(t):
                    return
                if positive(t):
                    gp.wait_ge(ctx_done, 2 * t)
                gp.tensor_tensor(BD[:, :, :].rearrange("p b (c d) -> p b c d", c=2),
                                 KR[:, bass.ds(2 * t, 2), :].unsqueeze(2).to_broadcast([P, 2, 2, DC]),
                                 HALF[:, :].unsqueeze(1).unsqueeze(3).to_broadcast([P, 2, 2, DC]),
                                 ALU.mult).then_inc(bd_ready, 1)

            def keys(t):
                if no_tile(t):
                    return
                if positive(t):
                    gp.wait_ge(s_done, 2 * t)
                gp.tensor_copy(KVS[:, :, :], KVT[:, bass.ds(2 * t, 2), :]).then_inc(keys_ready, 1)

            def rstd2(t):
                if no_tile(t):
                    return
                gp.wait_ge(l2_eps, t + 1)
                gp.tensor_tensor(RSTD2[:, :], VE2[:, :], MH[:, :], ALU.pow).then_inc(l2_rstd, 1)

            def step(i):
                rows_twice(i)
                rstd2(i - 1)
                keys(i + 1)

            gp.wait_ge(c_done, 4)
            gp.wait_ge(kvt_evac, 5)
            keys(0)
            step(0)
            with gp.Fori(1, T - 1) as i:
                step(i)
            step(T - 1)
            step(T)

            gp.wait_ge(row_stored, 16 * T)
            gp.wait_ge(weight_stored, 16 * T)
            gp.wait_ge(x1_stored, 16 * T)
            gp.wait_ge(zeroed, 16)

            gp.wait_ge(tab_ready, 2)
            used = tiles_used(mybir.EngineType.Pool)
            gp.wait_ge(slots_ready, 1)

            def met(*waits):
                waits = [(s, n if isinstance(n, int) else gp.to_reg(n)) for s, n in waits if positive(n)]
                gp.wait_ge(zeroed, 16)
                for s, n in waits:
                    gp.wait_ge(s, n)

            def gather(q, j, rows_of):
                k = j % UN
                g = UN * q + j
                if outside(g):
                    return
                met((xg_done, g - UN + 1), (wc_done, g - UN + 1), (idx_ready, g - AHEAD + 1))
                gp.indirect_dma_start(out=XG[:, k, :], out_offset=None, in_=rows,
                                      in_offset=bass.IndirectOffsetOnAxis(ap=rows_of, axis=0)).then_inc(gathered[k], 16)

            def add(q, j, rows_of):
                g = UN * q + j
                if outside(g):
                    return
                met((scaled, g + 1), (added[j % 2], nth_add(q, j - 2)))
                gp.indirect_dma_start(out=out if j % 2 == 0 else odd,
                                      out_offset=bass.IndirectOffsetOnAxis(ap=rows_of, axis=0),
                                      in_=YW[:, j % UN, :], in_offset=None, bounds_check=B * S - 1, oob_is_err=False,
                                      compute_op=ALU.add).then_inc(added[j % 2], 16)

            for j in range(AHEAD):
                gather(0, j, SLOT[:, j, 0:1])

            def steps(q, ks):
                for k in ks:
                    gather(q, k + AHEAD, IDX[:, k, 0:1])
                    add(q, k - BEHIND, IDX[:, k, 1:2])


            def tail(q, k):
                for j in (k, k + 1):
                    met((idx_ready, UN * q + j + 1))
                    add(q, j - BEHIND, IDX[:, j % UN, 1:2])
                met(*((added[j % 2], nth_add(q, j - BEHIND)) for j in (k, k + 1)))
                gp.dma_start(out.rearrange("(t p) i -> p t i", p=P), odd.rearrange("(t p) i -> p t i", p=P),
                             accum_op=ALU.add).then_inc(merged, 16)

            steps(0, range(UN))
            with gp.Fori(1, NG) as q:
                for k in range(UN):
                    with gp.If(used > UN * q + k):
                        steps(q, (k,))
                    with gp.If(used == UN * q + k):
                        tail(q, k)
            gp.wait_ge(merged, 16)

        @block.scalar
        def _(act):
            def evac(dst, src):
                return act.activation(dst, src, ACT.Copy)

            def rotated(g):
                h = slice(4 * g, 4 * g + 4)
                act.wait_ge(c_done, g + 1)
                evac(CA[:, h, :], bank[g % 2][:, 0:256].rearrange("p (h d) -> p h d", h=4)).then_inc(c_evac, 1)
                evac(CB[:, h, :], bank[g % 2][0:CQ - P, 256:512].rearrange("p (h d) -> p h d", h=4)).then_inc(c_evac, 1)

            def compressed(g):
                act.wait_ge(kt_done, g + 1)
                if g >= 2:
                    act.wait_ge(ek_done, g - 1)
                evac(EKT[:, g % 2, :, :], bank[2 + g % 2][:, 0:256].rearrange("p (q k) -> p q k", q=2)).then_inc(kt_evac, 1)

            def compressed_turned(g):
                act.wait_ge(ek_done, g + 1)
                evac(EK[:, 4 * g:4 * g + 4, :],
                     bank[2 + g % 2][:, 256:512].rearrange("p (h d) -> p h d", h=4)).then_inc(ek_evac, 1)

            def absorbed(g):
                act.wait_ge(mt2_done, g + 1)
                if g >= 2:
                    act.wait_ge(m_done, g - 1)
                evac(MT2[:, g % 2, :, :], bank[4 + g % 2][:, :].rearrange("p (q i) -> p q i", q=2)).then_inc(mt2_evac, 1)

            def turned(g):
                act.wait_ge(m_done, g + 1)
                evac(M[:, :, 4 * g:4 * g + 4, :],
                     bank[6 + g % 2][:, :].rearrange("p (c h d) -> p c h d", c=IC, h=4)).then_inc(m_evac, 1)

            for g in range(6):
                if g < 4:
                    rotated(g)
                if 2 <= g < 6:
                    compressed_turned(g - 2)
                if 1 <= g < 5:
                    compressed(g - 1)
                if 2 <= g < 6:
                    absorbed(g - 2)
                if 3 <= g < 6:
                    turned(g - 3)
            for lo, q, b, n in ((0, 0, 0, 8), (64, 0, 1, 8), (0, 1, 8, 8), (64, 1, 9, 7), (64, 1, 0, 1)):
                o = 0 if n > 1 else 7
                act.wait_ge(kvt_done, q + 1)
                evac(KVT[lo:lo + 64, b:b + n, :],
                     bank[q][lo:lo + 64, o * L:(o + n) * L].rearrange("p (b l) -> p b l", b=n)).then_inc(kvt_evac, 1)
            for q in range(4):
                act.wait_ge(xt_done, q + 1)
                evac(XNT[:, :, 2 * q * P:(2 * q + 2) * P],
                     bank[2 + q][:, :].rearrange("p (c n) -> p c n", c=IC)).then_inc(xt_evac, 1)
                if q == 0:
                    turned(3)
            act.wait_ge(setup, 2)

            def queries(t, g):
                if no_tile(t):
                    return
                act.wait_ge(g_done, 2 * t + g + 1)
                if positive(t):
                    act.wait_ge(s_done, 2 * t)
                evac(GQ[:, 4 * g:4 * g + 4, :], bank[g][:, :].rearrange("p (q n) -> p q n", q=4)).then_inc(g_evac, 1)

            def exp(t, b):
                if no_tile(t):
                    return
                act.wait_ge(max_done, 2 * t + b + 1)
                if positive(t):
                    act.wait_ge(pt_done, 2 * t + b - 1)
                for q in range(NP):
                    act.activation(PR[:, b, q, :], bank[2 + b][:, q * L:(q + 1) * L], ACT.Exp, bias=NM[:, b, q:q + 1],
                                   accum_out=SM[:, b, q:q + 1]).then_inc(exp_done, 1)

            def pt(t, b):
                if no_tile(t):
                    return
                act.wait_ge(pt_done, 2 * t + b + 1)
                if positive(t):
                    act.wait_ge(ctx_done, 2 * t + b - 1)
                evac(PT[:, b, :], bank[2 + b][:, :]).then_inc(pt_evac, 1)

            def latent(t, b):
                if no_tile(t):
                    return
                act.wait_ge(ctx_done, 2 * t + b + 1)
                if positive(t):
                    act.wait_ge(out_done, t)
                evac(CT[:, :, 64 * b:64 * b + 64], bank[4 + b][:, :].rearrange("p (q s) -> p q s", q=NP)).then_inc(ctx_evac, 1)

            def xt2(t):
                if no_tile(t):
                    return
                act.wait_ge(xt2_done, t + 1)
                if positive(t):
                    act.wait_ge(lg_done, t)
                evac(XN2C[:, :, :], bank[4][:, 0:D].rearrange("p (c n) -> p c n", c=IC)).then_inc(xt2_evac, 1)

            def top(t):
                if no_tile(t):
                    return
                act.wait_ge(rt, 6 * t + 2)
                act.activation(D4[:, :], D4[:, :], ACT.Exp, accum_out=S4[:, :]).then_inc(top_exp, 1)

            def step(i):
                xt2(i - 2)
                exp(i, 0)
                top(i - 2)
                exp(i, 1)
                pt(i, 0)
                queries(i + 1, 0)
                latent(i, 0)
                pt(i, 1)
                queries(i + 1, 1)
                latent(i, 1)

            queries(0, 0)
            queries(0, 1)
            for i in range(3):
                step(i)
            with act.Fori(3, T - 1) as i:
                step(i)
            for i in range(T - 1, T + 2):
                step(i)

            act.wait_ge(tab_ready, 2)
            used = tiles_used(mybir.EngineType.Activation)
            act.wait_ge(slots_ready, 2)

            def index(q, k):
                g = UN * q + k
                n = nth_add(q, k - UN - BEHIND)
                if positive(n):
                    act.wait_ge(added[k % 2], n)
                act.activation(IDX[:, k % UN, :], SLOT[:, bass.ds(g + AHEAD, 1), :].rearrange("p a i -> p (a i)"),
                               ACT.Copy).then_inc(idx_ready, 1)

            def rows_t(q, j):
                g = UN * q + j
                if outside(g):
                    return
                act.wait_ge(xg_done, g + 1)
                if positive(g - 1):
                    act.wait_ge(gu_done, g - 1)
                evac(XGT[:, j % 2, :, :], bank[j % 2][:, 0:IC * P].rearrange("p (c n) -> p c n", c=IC)).then_inc(xg_evac, 1)

            def silu(q, j):
                g = UN * q + j
                if outside(g):
                    return
                act.wait_ge(gu_done, g + 1)
                if positive(g - 1):
                    act.wait_ge(act_done, g - 1)
                act.activation(SG[:, j % 2, :], bank[2 + j % 2][:, 0:F], ACT.Silu).then_inc(silu_done, 1)

            def act_t(q, j):
                g = UN * q + j
                if outside(g):
                    return
                act.wait_ge(at_done, g + 1)
                if positive(g - 1):
                    act.wait_ge(y_done, g - 1)
                evac(ACT_T[:, j % 2, :, :], bank[4 + j % 2][0:FH, 0:2 * P].rearrange("p (c n) -> p c n", c=2)).then_inc(at_evac, 1)

            def steps(q, ks):
                for k in ks:
                    rows_t(q, k + 1)
                    index(q, k + 1)
                    silu(q, k)
                    act_t(q, k - 1)

            index(0, 0)
            rows_t(0, 0)

            def tail(q, k):
                act_t(q, k - 1)
                index(q, k + 1)

            steps(0, range(UN))
            with act.Fori(1, NG) as q:
                for k in range(UN):
                    with act.If(used > UN * q + k):
                        steps(q, (k,))
                    with act.If(used == UN * q + k):
                        tail(q, k)

        @block.vector
        def _(dve):
            def output_weights(j):
                dve.wait_ge(n_done, j + 1)
                dve.tensor_copy(N[:, 2 * j:2 * j + 2, :],
                                bank[(6, 7, 4, 5)[j]][:, :].rearrange("p (h o) -> p h o", h=2)).then_inc(n_evac, 1)

            output_weights(0)
            output_weights(1)
            dve.wait_ge(ld["x"], 16)
            for t in range(T):
                dve.bn_stats(ST6[:, t, :], X[:, t, :]).then_inc(ln_stats, 1)
            for t in range(T):
                dve.wait_ge(ln_stats, t + 1)
                dve.bn_aggr(MV[:, t, :], ST6[:, t, :]).then_inc(ln_aggr, 1)
            dve.wait_ge(ln_aggr, T)
            dve.tensor_scalar(VE[:, :], MV[:, :, 1], EPS, None, ALU.add).then_inc(ln_eps, 1)
            dve.wait_ge(ld["kv"], 16)
            dve.wait_ge(ld["const"], 16)
            hd = DC // 2
            for lo in (0, hd):
                src = hd - lo
                dve.tensor_tensor(KT1[:, :, lo:lo + hd], KVD[:, :, src:src + hd],
                                  RS[:, lo:lo + hd].unsqueeze(1).to_broadcast([P, B, hd]), ALU.mult).then_inc(ropa, 1)
            dve.tensor_tensor(KR[:, :, :], KVD[:, :, :], RC[:, :].unsqueeze(1).to_broadcast([P, B, DC]),
                              ALU.mult).then_inc(ropa, 1)
            dve.wait_ge(ropa, 3)
            dve.tensor_tensor(KR[:, :, :], KR[:, :, :], KT1[:, :, :], ALU.add).then_inc(ropc, 1)
            dve.wait_ge(ln_rstd, 1)
            for t in range(T):
                dve.tensor_scalar(XN[:, t, :], X[:, t, :], MV[:, t, 0:1], RSTD[:, t:t + 1],
                                  ALU.subtract, ALU.mult).then_inc(ln_done, 1)
            dve.wait_ge(setup, 2)

            def maximum(t, b):
                if no_tile(t):
                    return
                dve.wait_ge(s_done, 2 * t + b + 1)
                dve.tensor_reduce(NM[:, b, :], bank[2 + b][:, :].rearrange("p (q l) -> p q l", q=NP), AX.X, ALU.max,
                                  negate=True).then_inc(max_done, 1)

            def norm(t, b):
                if no_tile(t):
                    return
                u = 2 * t + b
                dve.wait_ge(exp_done, NP * (u + 1))
                dve.reciprocal(RI[:, b, :], SM[:, b, :]).then_inc(rcp_done, 1)
                dve.wait_ge(rcp_done, u + 1)
                dve.tensor_tensor(PR[:, b, :, :], PR[:, b, :, :], RI[:, b, :].unsqueeze(2).to_broadcast([P, NP, L]),
                                  ALU.mult).then_inc(norm_done, 1)

            def wait_alone(s, n):
                dve.wait_ge(setup, 2)
                dve.wait_ge(s, n)

            def residual(t):
                if no_tile(t):
                    return
                dve.wait_ge(out_done, t + 1)
                xt = X[:, bass.ds(t, 1), :].rearrange("p a i -> p (a i)")
                dve.tensor_tensor(xt, bank[6][:, 0:D], xt, ALU.add).then_inc(x1_done, 1)
                wait_alone(x1_done, t + 1)
                dve.bn_stats(ST62[:, :], xt).then_inc(l2_stats, 1)
                wait_alone(l2_stats, t + 1)
                dve.bn_aggr(MV2[:, :], ST62[:, :]).then_inc(l2_aggr, 1)
                dve.wait_ge(l2_aggr, t + 1)
                dve.tensor_scalar(VE2[:, :], MV2[:, 1:2], EPS, None, ALU.add).then_inc(l2_eps, 1)

            def norm2(t):
                if no_tile(t):
                    return
                dve.wait_ge(l2_rstd, t + 1)
                if positive(t):
                    dve.wait_ge(xt2_done, t)
                    dve.wait_ge(row_stored, 16 * t)
                xt = X[:, bass.ds(t, 1), :].rearrange("p a i -> p (a i)")
                dve.tensor_scalar(XN2[:, :], xt, MV2[:, 0:1], RSTD2[:, :], ALU.subtract, ALU.mult).then_inc(l2_done, 1)

            def router(t):
                if no_tile(t):
                    return
                r = 6 * t
                dve.wait_ge(lg_done, t + 1)
                dve.tensor_tensor(LG[:, :], bank[4][:, D:D + E], BI[:, :], ALU.add).then_inc(lg_read, 1)
                wait_alone(lg_read, t + 1)
                dve.max(M8[:, :], LG[:, :]).then_inc(rt, 1)
                dve.wait_ge(rt, r + 1)
                dve.tensor_scalar(D4[:, :], M8[:, 0:TOPK], M8[:, 0:1], None, ALU.subtract).then_inc(rt, 1)
                dve.max_index(I8[:, :], M8[:, :], LG[:, :]).then_inc(rt, 1)
                dve.wait_ge(rt, r + 3)
                dve.tensor_copy(I4F[:, :], I8[:, 0:TOPK]).then_inc(rt, 1)
                dve.wait_ge(rt, r + 4)
                if positive(t):
                    dve.wait_ge(wt_done, t)
                dve.tensor_tensor(OH[:, :, :], IOTA.unsqueeze(1).to_broadcast([P, TOPK, E]),
                                  I4F[:, :].unsqueeze(2).to_broadcast([P, TOPK, E]), ALU.is_equal).then_inc(rt, 1)
                dve.wait_ge(rt, r + 5)
                with nc.allow_low_precision(reason="a sum of at most one 1 is exact"):
                    dve.tensor_reduce(MT[:, :], OH[:, :, :].rearrange("p k e -> p e k"), AX.X, ALU.add).then_inc(mt_done, 1)

            def weights_scale(t):
                r = 6 * t
                dve.wait_ge(top_exp, t + 1)
                dve.reciprocal(R4[:, :], S4[:, :]).then_inc(rt, 1)
                dve.wait_ge(rt, r + 6)
                dve.tensor_scalar(W4[:, :], D4[:, :], R4[:, :], None, ALU.mult).then_inc(xtra, 1)

            def weights_place(t):
                dve.wait_ge(xtra, 2 * t + 1)
                dve.tensor_tensor(OW[:, :, :], OH[:, :, :], W4[:, :].unsqueeze(2).to_broadcast([P, TOPK, E]),
                                  ALU.mult).then_inc(xtra, 1)

            def weights_sum(t):
                dve.wait_ge(xtra, 2 * t + 2)
                if positive(t):
                    dve.wait_ge(weight_stored, 16 * t)
                dve.tensor_reduce(XE[:, D:XR], OW[:, :, :].rearrange("p k e -> p e k"), AX.X, ALU.add).then_inc(wt_done, 1)

            def weights(t):
                if no_tile(t):
                    return
                weights_scale(t)
                weights_place(t)
                weights_sum(t)

            def tally(t):
                if no_tile(t):
                    return
                r = 7 * t
                if positive(t):
                    dve.wait_ge(rk, r)
                dve.wait_ge(rk_done, t + 1)
                dve.tensor_tensor(RK[:, :], bank[5][:, 0:E], RUN[:, :], ALU.add).then_inc(rk, 1)
                dve.wait_ge(rk, r + 1)
                dve.tensor_tensor(RUN[:, :], bank[5][:, E:2 * E], RUN[:, :], ALU.add).then_inc(rk_read, 1)

            def rank_split(t):
                r = 7 * t
                dve.tensor_tensor(OR[:, :, :], OH[:, :, :], RK[:, :].unsqueeze(1).to_broadcast([P, TOPK, E]),
                                  ALU.mult).then_inc(rk, 1)
                dve.wait_ge(rk, r + 2)
                dve.tensor_reduce(RK4[:, :], OR[:, :, :], AX.X, ALU.add).then_inc(rk, 1)
                dve.wait_ge(rk, r + 3)
                dve.tensor_copy(RI4[:, :], RK4[:, :]).then_inc(rk, 1)
                dve.wait_ge(rk, r + 4)
                dve.tensor_scalar(J4[:, :], RI4[:, :], 7, None, ALU.arith_shift_right).then_inc(rk, 1)
                dve.tensor_scalar(S4I[:, :], RI4[:, :], P - 1, None, ALU.bitwise_and).then_inc(rk, 1)
                dve.wait_ge(rk, r + 6)
                dve.tensor_copy(S4F[:, :], S4I[:, :]).then_inc(rk, 1)
                dve.scalar_tensor_tensor(EJ4[:, :], I4F[:, :], float(T), J4[:, :], ALU.mult, ALU.add).then_inc(ej_done, 1)

            def rank_rows(t, k):
                if k == 0:
                    dve.wait_ge(rk, 7 * t + 7)
                    dve.wait_ge(inv_done, t + 1)
                    dve.wait_ge(ej_done, t + 1)
                dve.tensor_scalar(OHS[:, k, :], IOTAH[:, :], S4F[:, k:k + 1], None, ALU.is_equal).then_inc(ohs_done, 1)
                dve.tensor_scalar(VEJ[:, k, :], IOTAH[:, :], EJ4[:, k:k + 1], TOK[:, :],
                                  ALU.is_equal, ALU.mult).then_inc(ohs_done, 1)

            def rank(t):
                if no_tile(t):
                    return
                rank_split(t)
                for k in range(TOPK):
                    rank_rows(t, k)
                dve.wait_ge(ohs_done, 8 * t + 8)
                dve.tensor_scalar(TOK[:, :], TOK[:, :], float(P), None, ALU.add).then_inc(tok_done, 1)

            def step(i, first=False):
                rank(i - 3)
                maximum(i, 0)
                if first:
                    output_weights(2)
                router(i - 2)
                maximum(i, 1)
                if first:
                    output_weights(3)
                norm(i, 0)
                residual(i - 1)
                norm(i, 1)
                tally(i - 2)
                norm2(i - 1)
                weights(i - 2)

            dve.tensor_copy(IOTAH[:, :], CN[:, C_IOTA:C_IOTA + P]).then_inc(casts, 1)
            dve.tensor_copy(TRI[:, :], CN[:, C_TRI:C_TRI + P]).then_inc(casts, 1)
            dve.memset(ONES[:, :], 1.0).then_inc(casts, 1)
            dve.memset(RUN[:, :], 0.0).then_inc(casts, 1)
            dve.memset(SLOT[:, :, 0], 0).then_inc(casts, 1)
            dve.memset(SLOT[:, :, 1], NOWHERE).then_inc(casts, 1)
            dve.tensor_scalar(TOK[:, :], GCOL, 1.0, None, ALU.add).then_inc(casts, 1)
            dve.wait_ge(casts, 7)
            dve.wait_ge(ld["router"], 32)
            dve.sem_inc(inv_done, 1)
            for i in range(3):
                step(i, first=(i == 0))
            with dve.Fori(3, T - 1) as i:
                step(i)
            step(T - 1)
            rank(T - 3)
            router(T - 2)
            weights(T - 2)
            residual(T - 1)
            tally(T - 2)
            norm2(T - 1)
            rank(T - 2)
            router(T - 1)
            tally(T - 1)
            rank_split(T - 1)

            dve.wait_ge(rk_read, T)
            dve.tensor_tensor(CMP[:, :, :], RUN[:, :].unsqueeze(2).to_broadcast([P, E, T]),
                              STEP.unsqueeze(1).to_broadcast([P, E, T]), ALU.is_gt).then_inc(tb, 1)
            rank_rows(T - 1, 0)
            dve.wait_ge(tb, 1)
            dve.tensor_reduce(TE[:, :], CMP[:, :, :], AX.X, ALU.add).then_inc(tb, 1)
            rank_rows(T - 1, 1)
            dve.wait_ge(tb, 2)
            dve.tensor_tensor(CUM[:, :, :], TE[:, :].unsqueeze(1).to_broadcast([P, E, E]), UPTO, ALU.mult).then_inc(tb, 1)
            dve.tensor_scalar(TR[:, :], TE[:, :], -1.0, float(T), ALU.mult, ALU.add).then_inc(tb, 1)
            rank_rows(T - 1, 2)
            dve.wait_ge(tb, 4)
            dve.tensor_reduce(CI[:, :], CUM[:, :, :], AX.X, ALU.add).then_inc(tb, 1)
            rank_rows(T - 1, 3)
            dve.wait_ge(tb, 5)
            dve.scalar_tensor_tensor(FL[:, 1, :], CI[:, :], GCOL, TR[:, :], ALU.is_le, ALU.mult).then_inc(tb, 1)
            dve.tensor_scalar(FL[:, 0, :], CI[:, :], GCOL, None, ALU.is_le).then_inc(tb, 1)
            weights_scale(T - 1)
            dve.wait_ge(tb, 7)
            dve.tensor_reduce(EG[:, 0:2], FL[:, :, :], AX.X, ALU.add).then_inc(tb, 1)
            weights_place(T - 1)
            dve.wait_ge(tb, 8)
            dve.tensor_scalar(EG[:, 3:4], EG[:, 1:2], GCOL, float(P), ALU.add, ALU.min).then_inc(tb, 1)
            dve.tensor_scalar(EG[:, 2:3], EG[:, 0:1], float(E - 1), None, ALU.min).then_inc(tb, 1)
            weights_sum(T - 1)
            dve.wait_ge(tb, 10)
            dve.tensor_scalar(OHC[:, :], IOTAP, EG[:, 3:4], None, ALU.is_equal).then_inc(spread, 1)
            dve.wait_ge(inv_done, T + 1)
            dve.tensor_copy(INVT[:, :], bank[7][:, 0:P]).then_inc(spread, 1)
            dve.wait_ge(tab_done, 1)
            dve.tensor_copy(OHCT[:, :], bank[6][:, P:2 * P]).then_inc(spread, 1)
            dve.tensor_copy(TAB[:, 0:P - 1], bank[6][0:1, 0:P - 1]).then_inc(tab_ready, 1)
            dve.tensor_copy(TAB[:, P - 1:P], CI[0:1, E - 1:E]).then_inc(tab_ready, 1)
            dve.wait_ge(tab_done, 2)
            dve.tensor_scalar(SLOT[:, 0:NT, 0], bank[5][:, 0:NT], -1.0, 0.0, ALU.add, ALU.max).then_inc(slots_ready, 1)
            dve.tensor_scalar(INVZ[:, :], bank[5][:, 0:NT], 0.0, float(NOWHERE), ALU.is_equal, ALU.mult).then_inc(tb, 1)
            dve.wait_ge(tb, 11)
            dve.scalar_tensor_tensor(SLOT[:, AHEAD + BEHIND:AHEAD + BEHIND + NT, 1], bank[5][:, 0:NT], -1.0, INVZ[:, :],
                                     ALU.add, ALU.add).then_inc(slots_ready, 1)

            def weight(q, j, e):
                g = UN * q + j
                if outside(g):
                    return
                dve.wait_ge(gathered[j % UN], nth_gather(q, j))
                if positive(g - UN + 1):
                    dve.wait_ge(scaled, g - UN + 1)
                dve.tensor_copy(WC[:, j % UN:j % UN + 1], XG[:, j % UN, bass.ds(D + e, 1)]).then_inc(wc_done, 1)

            def product(q, j):
                g = UN * q + j
                if outside(g):
                    return
                dve.wait_ge(silu_done, g + 1)
                if positive(g - 1):
                    dve.wait_ge(at_done, g - 1)
                dve.tensor_tensor(AC[:, j % 2, :], SG[:, j % 2, :], bank[2 + j % 2][:, F:2 * F], ALU.mult).then_inc(act_done, 1)

            def weigh(q, j):
                g = UN * q + j
                if outside(g):
                    return
                dve.wait_ge(y_done, g + 1)
                dve.wait_ge(wc_done, g + 1)
                if positive(nth_add(q, j - UN)):
                    dve.wait_ge(added[j % 2], nth_add(q, j - UN))
                dve.tensor_scalar(YW[:, j % UN, :], bank[6 + j % 2][:, 0:D], WC[:, j % UN:j % UN + 1], None,
                                  ALU.mult).then_inc(scaled, 1)

            def steps(q, ks):
                e = experts(mybir.EngineType.DVE, UN * q + ks[0] + 1, len(ks))
                for k in ks:
                    weight(q, k + 1, e[k - ks[0]])
                    product(q, k)
                    weigh(q, k - BEHIND)

            weight(0, 0, experts(mybir.EngineType.DVE, 0, 1)[0])
            used = tiles_used(mybir.EngineType.DVE)

            def tail(q, k):
                weigh(q, k - 2)
                weigh(q, k - 1)

            steps(0, range(UN))
            with dve.Fori(1, NG) as q:
                for k in range(UN):
                    with dve.If(used > UN * q + k):
                        steps(q, (k,))
                    with dve.If(used == UN * q + k):
                        tail(q, k)

        @block.tensor
        def _(pe):
            def rotated(g):
                pe.wait_ge(ld["qr"], 32)
                if g >= 2:
                    pe.wait_ge(c_evac, 2 * g - 2)
                for h in range(4 * g, 4 * g + 4):
                    o = (h % 4) * DC
                    pe.matmul(bank[g % 2][:, o:o + DC], WQR[:, h, 0:P], WKR[:, h, :], start=True, stop=True)
                    last = pe.matmul(bank[g % 2][0:CQ - P, 256 + o:256 + o + DC], WQR[:, h, P:CQ], WKR[:, h, :],
                                     start=True, stop=True)
                last.then_inc(c_done, 1)

            def compressed(g):
                pe.wait_ge(ld[f"kc{g // 2}"], 32)
                pe.wait_ge(c_evac, 2 * g + 2)
                if g >= 2:
                    pe.wait_ge(ek_evac, g - 1)
                for q in range(2):
                    for stat, mov in ((CA, KCA), (CB, KCB)):
                        for h2 in range(2):
                            h = 4 * g + 2 * q + h2
                            last = pe.matmul(bank[2 + g % 2][64 * h2:64 * h2 + 64, q * P:(q + 1) * P], stat[:, h, :],
                                             mov[:, h, :], start=(stat is CA), stop=(stat is CB))
                last.then_inc(kt_done, 1)

            def compressed_turned(g):
                pe.wait_ge(ld["const"], 16)
                pe.wait_ge(kt_evac, g + 1)
                for q in range(2):
                    last = pe.transpose(bank[2 + g % 2][:, 256 + q * P:256 + (q + 1) * P], EKT[:, g % 2, q, :], IDN)
                last.then_inc(ek_done, 1)

            def absorbed(g):
                pe.wait_ge(ld[f"wq{g // 2}"], 16)
                pe.wait_ge(ek_evac, g + 1)
                if g >= 2:
                    pe.wait_ge(mt2_evac, g - 1)
                for h in range(4 * g, 4 * g + 4):
                    q, h2 = h % 4 // 2, h % 2
                    last = pe.matmul(bank[4 + g % 2][64 * h2:64 * h2 + 64, q * D:(q + 1) * D], EK[:, h, :], WQ[:, h, :],
                                     start=True, stop=True)
                last.then_inc(mt2_done, 1)

            def turned(g):
                pe.wait_ge(ld["const"], 16)
                pe.wait_ge(mt2_evac, g + 1)
                if g >= 2:
                    pe.wait_ge(m_evac, g - 1)
                else:
                    pe.wait_ge(n_evac, g + 1)
                for c in range(IC):
                    for q in range(2):
                        o = (2 * c + q) * P
                        last = pe.transpose(bank[6 + g % 2][:, o:o + P], MT2[:, g % 2, q, c * P:(c + 1) * P], IDN)
                last.then_inc(m_done, 1)

            def output_weights(j):
                pe.wait_ge(ld["kckv"], 16)
                pe.wait_ge(ld[f"wo{j // 2}"], 16)
                if j >= 2:
                    pe.wait_ge(xt_evac, 4)
                for p2 in range(2):
                    for h2 in range(2):
                        h = 4 * j + 2 * p2 + h2
                        last = pe.matmul(bank[(6, 7, 4, 5)[j]][64 * p2:64 * p2 + 64, h2 * D:(h2 + 1) * D], KCKV[:, h, :],
                                         WO[:, h, :], start=True, stop=True)
                last.then_inc(n_done, 1)

            output_weights(0)
            output_weights(1)
            for g in range(6):
                if g < 4:
                    rotated(g)
                if 2 <= g < 6:
                    compressed_turned(g - 2)
                if 1 <= g < 5:
                    compressed(g - 1)
                if 2 <= g < 6:
                    absorbed(g - 2)
                if 3 <= g < 6:
                    turned(g - 3)
            pe.wait_ge(ropc, 1)
            pe.wait_ge(c_evac, 8)
            for b in range(B):
                o = slice((b % 8) * L, (b % 8 + 1) * L)
                if b < B - 1:
                    last = pe.matmul(bank[b // 8][:, o], KR[0:64, b:b + 2, :].rearrange("p b d -> p (b d)"),
                                     IDN[0:64, 0:64], start=True, stop=True)
                else:
                    pe.matmul(bank[1][0:64, o], KR[0:64, b, :], IDN[0:64, 0:64], start=True, stop=True)
                    last = pe.matmul(bank[1][64:128, o], KR[64:128, 0, :], IDN[64:128, 64:128], start=True, stop=True)
                if b % 8 == 7:
                    last.then_inc(kvt_done, 1)
            pe.wait_ge(ek_evac, 4)
            pe.wait_ge(mt2_evac, 4)
            for t in range(T):
                pe.wait_ge(ln_done, t + 1)
                for c in range(IC):
                    last = pe.transpose(bank[2 + t // 2][:, c * 2 * P + (t % 2) * P:c * 2 * P + (t % 2 + 1) * P],
                                        XN[:, t, c * P:(c + 1) * P], IDN)
                if t % 2:
                    last.then_inc(xt_done, 1)
                if t == 1:
                    turned(3)

            def query(t, g, q):
                if no_tile(t):
                    return
                if q == 0 and positive(t):
                    pe.wait_ge(g_evac, 2 * t + g - 1)
                h = 8 * g + 2 * q
                for c in range(IC):
                    last = pe.matmul(bank[g][:, q * P:(q + 1) * P], M[:, c, h:h + 2, :].rearrange("p h d -> p (h d)"),
                                     XNT[:, c, bass.ts(t, P)], start=(c == 0), stop=(c == IC - 1))
                if q == 3:
                    last.then_inc(g_done, 1)

            def score(t, b, q):
                if no_tile(t):
                    return
                waits = []
                if q == 0 and positive(t):
                    waits.append((pt_evac, 2 * t + b - 1))
                if b == 0 and q in (0, 4):
                    waits.append((g_evac, 2 * t + 1 + q // 4))
                if b == 0 and q == 0:
                    waits.append((keys_ready, t + 1))
                if waits:
                    waits = [(s, n if isinstance(n, int) else pe.to_reg(n)) for s, n in waits]
                    pe.wait_ge(ld["qr"], 32)
                    for s, n in waits:
                        pe.wait_ge(s, n)
                for lo in (0, 64):
                    m = pe.matmul(bank[2 + b][lo:lo + 64, q * L:(q + 1) * L], GQ[lo:lo + 64, q, 64 * b:64 * b + 64],
                                  KVS[lo:lo + 64, b, :], start=True, stop=True)
                if q == NP - 1:
                    m.then_inc(s_done, 1)

            def transposed(t, b):
                if no_tile(t):
                    return
                pe.wait_ge(norm_done, 2 * t + b + 1)
                for j in range(4):
                    last = pe.transpose(bank[2 + b][:, j * P:(j + 1) * P],
                                        PR[:, b, 2 * j:2 * j + 2, :].rearrange("p q l -> p (q l)"), IDN)
                last.then_inc(pt_done, 1)

            def attend(t, b):
                if no_tile(t):
                    return
                pe.wait_ge(pt_evac, 2 * t + b + 1)
                pe.wait_ge(bd_ready, t + 1)
                if positive(t):
                    pe.wait_ge(ctx_evac, 2 * t + b - 1)
                if positive(t - 1):
                    pe.wait_ge((lg_read, rk_read)[b], t - 1)
                pe.matmul(bank[4 + b][:, :], BD[:, b, :], PT[:, b, :], start=True, stop=True).then_inc(ctx_done, 1)

            def project(t, q):
                if no_tile(t):
                    return
                if q == 0:
                    pe.wait_ge(ctx_evac, 2 * t + 2)
                    if positive(t):
                        pe.wait_ge(x1_done, t)
                m = pe.matmul(bank[6][:, 0:D], CT[:, q, :], N[:, q, :], start=(q == 0), stop=(q == NP - 1))
                if q == NP - 1:
                    m.then_inc(out_done, 1)

            def latents(t, b):
                return 2 * min(t, T - 1) + b + 1 if isinstance(t, int) else 2 * t + b + 1

            def route(t):
                if no_tile(t):
                    return
                pe.wait_ge(l2_done, t + 1)
                pe.wait_ge(ctx_evac, latents(t + 1, 0))
                if positive(t):
                    pe.wait_ge(lg_read, t)
                for c in range(IC):
                    last = pe.transpose(bank[4][:, c * P:(c + 1) * P], XN2[:, c * P:(c + 1) * P], IDN)
                last.then_inc(xt2_done, 1)

            def logits(t):
                if no_tile(t):
                    return
                pe.wait_ge(xt2_evac, t + 1)
                for c in range(IC):
                    last = pe.matmul(bank[4][:, D:D + E], XN2C[:, c, :], RW[:, c, :], start=(c == 0), stop=(c == IC - 1))
                last.then_inc(lg_done, 1)

            def ranks(t):
                if no_tile(t):
                    return
                pe.wait_ge(mt_done, t + 1)
                pe.wait_ge(ctx_evac, latents(t + 1, 1))
                if positive(t):
                    pe.wait_ge(rk_read, t)
                pe.matmul(bank[5][:, 0:E], TRI[:, :], MT[:, :], start=True, stop=True)
                pe.matmul(bank[5][:, E:2 * E], ONES[:, :], MT[:, :], start=True, stop=True).then_inc(rk_done, 1)

            def invert(t):
                if no_tile(t):
                    return
                first, last = isinstance(t, int) and t == 0, isinstance(t, int) and t == T - 1
                pe.wait_ge(ohs_done, 8 * t + 8)
                for k in range(TOPK):
                    m = pe.matmul(bank[7][:, 0:P], VEJ[:, k, :], OHS[:, k, :], start=(first and k == 0),
                                  stop=(last and k == TOPK - 1))
                m.then_inc(inv_done, 1)

            def step(i, first=False):
                for q in range(NP):
                    score(i, 0, q)
                    if q % 2:
                        query(i + 1, 0, q // 2)
                    if q == 3:
                        route(i - 2)
                logits(i - 2)
                if first:
                    output_weights(2)
                for q in range(NP):
                    score(i, 1, q)
                    if q % 2:
                        project(i - 1, q // 2)
                if first:
                    output_weights(3)
                    pe.wait_ge(n_evac, 4)
                for q in range(NP // 2, NP):
                    project(i - 1, q)
                ranks(i - 2)
                invert(i - 3)
                transposed(i, 0)
                query(i + 1, 1, 0)
                query(i + 1, 1, 1)
                attend(i, 0)
                transposed(i, 1)
                query(i + 1, 1, 2)
                query(i + 1, 1, 3)
                attend(i, 1)

            pe.wait_ge(setup, 2)
            pe.wait_ge(ld["router"], 32)
            for g in range(2):
                pe.wait_ge(m_evac, 2 * g + 2)
                pe.wait_ge(xt_evac, 1)
                pe.wait_ge(kvt_evac, 5)
                for q in range(4):
                    query(0, g, q)
            for i in range(4):
                step(i, first=(i == 0))
            with pe.Fori(4, T - 1) as i:
                step(i)
            for i in range(T - 1, T + 3):
                step(i)
            pe.wait_ge(tb, 10)
            pe.matmul(bank[6][0:1, 0:P], EG[:, 2:3], IDN, start=True, stop=True)
            pe.wait_ge(spread, 1)
            pe.transpose(bank[6][:, P:2 * P], OHC[:, :], IDN).then_inc(tab_done, 1)
            pe.wait_ge(spread, 3)
            pe.matmul(bank[5][:, 0:NT], INVT[:, :], OHCT[:, 0:NT], start=True, stop=True).then_inc(tab_done, 1)
            for _ in range(5):
                pe.matmul(bank[7][:, 0:D], ZERO[:, 0:P], ZERO[:, :], start=True, stop=True)
            pe.wait_ge(tab_ready, 2)
            pe.wait_ge(ld["wgu"], 16)
            pe.wait_ge(ld["wd"], 16)

            def turn(q, j):
                g = UN * q + j
                if outside(g):
                    return
                pe.wait_ge(gathered[j % UN], nth_gather(q, j))
                if positive(g - 1):
                    pe.wait_ge(xg_evac, g - 1)
                for c in range(IC):
                    last = pe.transpose(bank[j % 2][:, c * P:(c + 1) * P], XG[:, j % UN, c * P:(c + 1) * P], IDN)
                last.then_inc(xg_done, 1)

            def gate_up(q, j, e):
                g = UN * q + j
                if outside(g):
                    return
                pe.wait_ge(xg_evac, g + 1)
                if positive(g - 1):
                    pe.wait_ge(act_done, g - 1)
                for c in range(IC):
                    last = pe.matmul(bank[2 + j % 2][:, 0:2 * F], XGT[:, j % 2, c, :],
                                     WGU[:, bass.ds(e, 1), c, :].rearrange("p a f -> p (a f)"),
                                     start=(c == 0), stop=(c == IC - 1))
                last.then_inc(gu_done, 1)

            def turn_act(q, j):
                g = UN * q + j
                if outside(g):
                    return
                pe.wait_ge(act_done, g + 1)
                if positive(g - 1):
                    pe.wait_ge(at_evac, g - 1)
                for c in range(2):
                    last = pe.transpose(bank[4 + j % 2][0:FH, c * P:(c + 1) * P], AC[:, j % 2, c * FH:(c + 1) * FH], IDN)
                last.then_inc(at_done, 1)

            def down(q, j, e):
                g = UN * q + j
                if outside(g):
                    return
                pe.wait_ge(at_evac, g + 1)
                if positive(g - 1):
                    pe.wait_ge(scaled, g - 1)
                for c in range(2):
                    last = pe.matmul(bank[6 + j % 2][:, 0:D], ACT_T[:, j % 2, c, :],
                                     WD[:, bass.ds(e, 1), c, :].rearrange("p a f -> p (a f)"),
                                     start=(c == 0), stop=(c == 1))
                last.then_inc(y_done, 1)

            def steps(q, ks, skip=0):
                e = [None] * skip + experts(mybir.EngineType.PE, UN * q + ks[0] - BEHIND + skip, len(ks) + BEHIND - skip)
                for k in ks:
                    turn(q, k + 1)
                    gate_up(q, k, e[k - ks[0] + BEHIND])
                    turn_act(q, k - 1)
                    down(q, k - BEHIND, e[k - ks[0]])

            turn(0, 0)
            used = tiles_used(mybir.EngineType.PE)

            def tail(q, k):
                e = experts(mybir.EngineType.PE, UN * q + k - BEHIND, BEHIND)
                turn_act(q, k - 1)
                down(q, k - 2, e[0])
                down(q, k - 1, e[1])

            steps(0, range(UN), skip=BEHIND)
            with pe.Fori(1, NG) as q:
                for k in range(UN):
                    with pe.If(used > UN * q + k):
                        steps(q, (k,))
                    with pe.If(used == UN * q + k):
                        tail(q, k)


_OUT = ((B, S, D), "float32")


def kernel(**inputs):
    import concourse.bacc as bacc
    from concourse.bass_utils import run_bass_kernel_spmd

    a = {k: np.asarray(v) for k, v in inputs.items()}

    def w(name):
        return a["L0_xattn_" + name]

    def f(name):
        return a["L0_ffn_" + name]

    inv = (np.float32(1.0) / np.float32(10000.0) ** (np.arange(0, DC, 2, dtype=np.float32) / np.float32(DC))).astype(np.float32)
    ang = np.arange(L, dtype=np.float32)[:, None] * inv[None, :]
    cos = np.repeat(np.cos(ang), 2, axis=-1).astype(np.float32)
    sin = np.repeat(np.sin(ang), 2, axis=-1).astype(np.float32)
    sin[:, :DC // 2] *= -1.0
    upto = np.tril(np.ones((E, E), np.float32))
    ahead = np.triu(np.ones((P, P), np.float32), 1)
    const = np.concatenate([np.eye(P, dtype=np.float32), np.concatenate([cos, cos]), np.concatenate([sin, sin]),
                            np.repeat(np.eye(2, dtype=np.float32), P // 2, axis=0),
                            np.tile(np.arange(P, dtype=np.float32), (P, 1)),
                            np.tile(np.arange(T, dtype=np.float32) * P, (P, 1)),
                            np.tile(upto.reshape(1, E * E), (P, 1)),
                            np.arange(P, dtype=np.float32).reshape(P, 1), ahead], axis=1)
    kvd = a["ctx_512"].transpose(1, 0, 2)
    arrays = {
        "x": a["x"].reshape(T, P, D).transpose(1, 0, 2),
        "ctxd": np.concatenate([kvd, kvd], axis=0),
        "const": const,
        "wqrT": w("W_qr").transpose(2, 0, 1),
        "wkrT": w("W_kr").transpose(2, 0, 1),
        "kcqT_a": w("w_kc_q").transpose(2, 0, 1)[:P],
        "kcqT_b": w("w_kc_q").transpose(2, 0, 1)[P:],
        "wq": w("Wq").reshape(H, K, D).transpose(1, 0, 2),
        "kckv": w("w_kc_kv").transpose(1, 0, 2),
        "woT": w("Wo").reshape(D, H, K).transpose(2, 1, 0),
        "rwT": f("router_w").reshape(E, IC, P).transpose(2, 1, 0),
        "bias": np.concatenate([f("expert_bias").reshape(1, E)] * P, axis=0),
        "wgu": np.concatenate([f("gate_proj"), f("up_proj")], axis=2).reshape(E, IC, P, 2 * F).transpose(2, 0, 1, 3),
        "wd": f("down_proj").reshape(E, 2, FH, D).transpose(2, 0, 1, 3),
    }
    arrays = {k: np.ascontiguousarray(v) for k, v in arrays.items()}
    nc = bacc.Bacc("TRN2", target_bir_lowering=False, num_devices=1)
    args = [nc.dram_tensor(k, v.shape, mybir.dt.from_np(v.dtype), kind="ExternalInput").ap() for k, v in arrays.items()]
    res = nc.dram_tensor("out", (B * S, D), F32, kind="ExternalOutput").ap()
    build(nc, *args, res)
    r = run_bass_kernel_spmd(nc, [arrays], core_ids=[0])
    return r.results[0]["out"].reshape(B, S, D)
```
